# Optimizing a Trainium2 kernel written in Bass

```python
import numpy as np
import jax
import jax.numpy as jnp

def _softmax(x, axis=-1):
    return jax.nn.softmax(x, axis=axis)

def _gelu(x):
    return jax.nn.gelu(x, approximate=True)

def _silu(x):
    return jax.nn.silu(x)

def _sigmoid(x):
    return jax.nn.sigmoid(x)

def _layernorm(x, axis=-1, eps=1e-05):
    m = jnp.mean(x, axis=axis, keepdims=True)
    v = jnp.var(x, axis=axis, keepdims=True)
    return (x - m) / jnp.sqrt(v + eps)

def _scatter_add(tgt, idx, src, axis=0):
    return tgt.at[idx].add(src)

def _segment_sum(src, seg, n):
    return jax.ops.segment_sum(src, seg, n)
kernel_name = 'mk_decoder_postln_d1_seqx_r2_3d63c7'

def setup_inputs(seed: int=0):
    np.random.seed(seed)
    _w = jnp.asarray

    def _rec_inputs():
        import jax
        import jax.numpy as jnp
        _rk = jax.random.key(seed)
        x = 7.22e-05 + 1 * jax.random.normal(jax.random.fold_in(_rk, 1), (8, 512, 512), jnp.float32)
        _lenS = 512 - jax.random.randint(jax.random.fold_in(_rk, 7), (8,), 0, max(1, 512 // 4) + 1, jnp.int32)
        _lenS2 = 512 - jax.random.randint(jax.random.fold_in(_rk, 8), (8,), 0, max(1, 512 // 4) + 1, jnp.int32)
        _ctx_1024P = jax.random.normal(jax.random.fold_in(_rk, 11), (8, 16, 512), jnp.float32)
        _ctx_1024c = jax.random.dirichlet(jax.random.fold_in(_rk, 511), 0.3 * jnp.ones((16,), jnp.float32), (8, 512))
        _ctx_1024t = jnp.einsum('bsk,bkd->bsd', _ctx_1024c, _ctx_1024P)
        _ctx_1024t = _ctx_1024t * jax.lax.rsqrt(jnp.mean(jnp.square(_ctx_1024t)) + 1e-12) * 0.953939
        ctx_1024 = 4.13588e-05 + 0.999923 * (_ctx_1024t + 0.3 * jax.random.normal(jax.random.fold_in(_rk, 611), (8, 512, 512), jnp.float32))
        itok_Sx12_0_8189 = jax.random.randint(jax.random.fold_in(_rk, 12), (512, 12), 0, 4095, jnp.int32)
        _validS = jnp.arange(512)[None, :] < _lenS[:, None]
        _validS2 = jnp.arange(512)[None, :] < _lenS2[:, None]
        _causal = jnp.tril(jnp.ones((512, 512), dtype=bool))
        mask_Sx12_bk0 = jnp.logical_not(jnp.ones((512, 12), dtype=bool))
        return (x, ctx_1024, itok_Sx12_0_8189, mask_Sx12_bk0)
    x, ctx_1024, itok_Sx12_0_8189, mask_Sx12_bk0 = _rec_inputs()

    def _L0_attn_setup():
        import jax, jax.numpy as jnp
        import numpy as np
        import math
        B, T, E, H = (2, 1024, 512, 16)
        D = E // H
        THETA = 10000.0

        def _rope(x):
            d = x.shape[-1]
            t = x.shape[1]
            freqs = 1.0 / THETA ** (jnp.arange(0, d, 2, dtype=jnp.float32) / d)
            ang = jnp.arange(t, dtype=jnp.float32)[:, None] * freqs[None, :]
            cos = jnp.cos(ang)[None, :, None, :]
            sin = jnp.sin(ang)[None, :, None, :]
            xr = x[..., 0::2]
            xi = x[..., 1::2]
            o = jnp.stack([xr * cos - xi * sin, xr * sin + xi * cos], axis=-1)
            return o.reshape(x.shape)
        key = jax.random.key(seed)
        k1, k2, k3 = jax.random.split(key, 3)
        x = jax.random.normal(k1, (B, T, E), dtype=jnp.float32)
        W_qkv = jax.random.normal(k2, (3 * E, E), dtype=jnp.float32) * 0.02
        b_qkv = jax.random.normal(k3, (3 * E,), dtype=jnp.float32) * 0.02
        return {'x': x, 'W_qkv': W_qkv, 'b_qkv': b_qkv}
    _L0_attn_all = _L0_attn_setup()
    _L0_attn_in = {k: v for k, v in _L0_attn_all.items() if k in ('W_qkv', 'b_qkv')}
    del _L0_attn_all

    def _L0_xattn_setup():
        import jax, jax.numpy as jnp
        import numpy as np
        import math
        B, L, D, H = (2, 2048, 512, 16)
        DH = D // H

        def _build_table(seq_len):
            assert seq_len & seq_len - 1 == 0
            levels = int(math.log2(seq_len))
            max_valid = 2 * seq_len - 3
            idx = np.full((seq_len, levels), -1, dtype=np.int64)
            cm = np.zeros((seq_len, levels), dtype=bool)
            for n in range(seq_len):
                c = n
                for lvl in range(levels):
                    if lvl == 0:
                        nxt = c ^ 1
                        pair = c
                    else:
                        nxt = c // 2 + seq_len ^ 1
                        pair = c // 2 + seq_len
                    if nxt > max_valid:
                        break
                    if pair < nxt:
                        cm[n, lvl] = True
                    idx[n, lvl] = nxt
                    c = nxt
            return (idx, cm)
        rng = jax.random.key(seed)
        ks = jax.random.split(rng, 8)
        s = 0.02
        idx, cm = _build_table(L)
        return {'query': jax.random.normal(ks[0], (B, L, D), jnp.float32), 'key': jax.random.normal(ks[1], (B, L, D), jnp.float32), 'value': jax.random.normal(ks[2], (B, L, D), jnp.float32), 'Wq': jax.random.normal(ks[3], (D, D), jnp.float32) * s, 'Wk': jax.random.normal(ks[4], (D, D), jnp.float32) * s, 'Wv': jax.random.normal(ks[5], (D, D), jnp.float32) * s, 'Wo': jax.random.normal(ks[6], (D, D), jnp.float32) * s, 'bo': jax.random.normal(ks[7], (D,), jnp.float32) * s, 'idx_table': jnp.asarray(idx), 'causal_mask': jnp.asarray(cm)}
    _L0_xattn_all = _L0_xattn_setup()
    _L0_xattn_in = {k: v for k, v in _L0_xattn_all.items() if k in ('Wq', 'Wk', 'Wv', 'Wo', 'bo')}
    del _L0_xattn_all

    def _L0_ffn_setup():
        import jax, jax.numpy as jnp
        import numpy as np
        B, S, D = (4, 1024, 512)
        N_EXPERTS, EXPERT_SIZE = (16, 128)
        WIDTH = N_EXPERTS * EXPERT_SIZE
        key = jax.random.key(seed)
        k_x, k_w1, k_w2, k_g = jax.random.split(key, 4)
        x = jax.random.normal(k_x, (B, S, D), dtype=jnp.float32)
        w1 = jax.random.normal(k_w1, (D, WIDTH), dtype=jnp.float32) / np.sqrt(D).astype(np.float32)
        b1 = jnp.zeros((WIDTH,), dtype=jnp.float32)
        w2 = jax.random.normal(k_w2, (WIDTH, D), dtype=jnp.float32) / np.sqrt(WIDTH).astype(np.float32)
        b2 = jnp.zeros((D,), dtype=jnp.float32)
        return {'x': x, 'w1': w1, 'b1': b1, 'w2': w2, 'b2': b2}
    _L0_ffn_all = _L0_ffn_setup()
    _L0_ffn_in = {k: v for k, v in _L0_ffn_all.items() if k in ('w1', 'b1', 'w2', 'b2')}
    del _L0_ffn_all
    return {'x': x, 'ctx_1024': ctx_1024, 'itok_Sx12_0_8189': itok_Sx12_0_8189, 'mask_Sx12_bk0': mask_Sx12_bk0, 'L0_attn_W_qkv': _L0_attn_in['W_qkv'], 'L0_attn_b_qkv': _L0_attn_in['b_qkv'], 'L0_xattn_Wq': _L0_xattn_in['Wq'], 'L0_xattn_Wk': _L0_xattn_in['Wk'], 'L0_xattn_Wv': _L0_xattn_in['Wv'], 'L0_xattn_Wo': _L0_xattn_in['Wo'], 'L0_xattn_bo': _L0_xattn_in['bo'], 'L0_ffn_w1': _L0_ffn_in['w1'], 'L0_ffn_b1': _L0_ffn_in['b1'], 'L0_ffn_w2': _L0_ffn_in['w2'], 'L0_ffn_b2': _L0_ffn_in['b2']}

def reference(x, ctx_1024, itok_Sx12_0_8189, mask_Sx12_bk0, L0_attn_W_qkv, L0_attn_b_qkv, L0_xattn_Wq, L0_xattn_Wk, L0_xattn_Wv, L0_xattn_Wo, L0_xattn_bo, L0_ffn_w1, L0_ffn_b1, L0_ffn_w2, L0_ffn_b2):
    import jax
    import jax.numpy as jnp

    def _L0_attn_ref(x, W_qkv, b_qkv):
        import jax, jax.numpy as jnp
        import numpy as np
        import math
        B, T, E, H = (2, 1024, 512, 16)
        D = E // H
        THETA = 10000.0

        def _rope(x):
            d = x.shape[-1]
            t = x.shape[1]
            freqs = 1.0 / THETA ** (jnp.arange(0, d, 2, dtype=jnp.float32) / d)
            ang = jnp.arange(t, dtype=jnp.float32)[:, None] * freqs[None, :]
            cos = jnp.cos(ang)[None, :, None, :]
            sin = jnp.sin(ang)[None, :, None, :]
            xr = x[..., 0::2]
            xi = x[..., 1::2]
            o = jnp.stack([xr * cos - xi * sin, xr * sin + xi * cos], axis=-1)
            return o.reshape(x.shape)
        b, t, _ = x.shape
        qkv = x @ W_qkv.T + b_qkv
        qkv = qkv.reshape(b, t, 3, H, D)
        q, k, v = (qkv[:, :, 0], qkv[:, :, 1], qkv[:, :, 2])
        q = _rope(q)
        k = _rope(k)
        q = q.transpose(0, 2, 1, 3)
        k = k.transpose(0, 2, 1, 3)
        v = v.transpose(0, 2, 1, 3)
        scores = jnp.einsum('bhqd,bhkd->bhqk', q, k) / math.sqrt(D)
        w = jax.nn.softmax(scores, axis=-1)
        out = jnp.einsum('bhqk,bhkd->bhqd', w, v)
        return out.transpose(0, 2, 1, 3).reshape(b, t, E)

    def _L0_xattn_ref(query, key, value, Wq, Wk, Wv, Wo, bo, idx_table, causal_mask):
        import jax, jax.numpy as jnp
        import numpy as np
        import math
        B, L, D, H = (2, 2048, 512, 16)
        DH = D // H

        def _build_table(seq_len):
            assert seq_len & seq_len - 1 == 0
            levels = int(math.log2(seq_len))
            max_valid = 2 * seq_len - 3
            idx = np.full((seq_len, levels), -1, dtype=np.int64)
            cm = np.zeros((seq_len, levels), dtype=bool)
            for n in range(seq_len):
                c = n
                for lvl in range(levels):
                    if lvl == 0:
                        nxt = c ^ 1
                        pair = c
                    else:
                        nxt = c // 2 + seq_len ^ 1
                        pair = c // 2 + seq_len
                    if nxt > max_valid:
                        break
                    if pair < nxt:
                        cm[n, lvl] = True
                    idx[n, lvl] = nxt
                    c = nxt
            return (idx, cm)
        Bq, Lq, Dm = query.shape
        scale = 1.0 / math.sqrt(DH)

        def heads(x, W):
            return (x @ W.T).reshape(Bq, Lq, H, DH).transpose(0, 2, 1, 3)
        Q = heads(query, Wq)
        K = heads(key, Wk)
        V = heads(value, Wv)
        Ks, Vs = ([K], [V])
        while Ks[-1].shape[2] > 1:
            k, v = (Ks[-1], Vs[-1])
            Lc = k.shape[2]
            k2 = k.reshape(Bq, H, Lc // 2, 2, DH)
            v2 = v.reshape(Bq, H, Lc // 2, 2, DH)
            Ks.append(0.5 * (k2[:, :, :, 0] + k2[:, :, :, 1]))
            Vs.append(v2[:, :, :, 0] + v2[:, :, :, 1])
        flatK = jnp.concatenate(Ks, axis=2)
        flatV = jnp.concatenate(Vs, axis=2)
        nk = flatK[:, :, idx_table]
        nv = flatV[:, :, idx_table]
        self_logits = jnp.einsum('bhnd,bhnd->bhn', Q, K) * scale
        nbr_logits = jnp.einsum('bhld,bhlnd->bhln', Q, nk) * scale
        nbr_logits = jnp.where(causal_mask[None, None], -jnp.inf, nbr_logits)
        all_logits = jnp.concatenate([self_logits[..., None], nbr_logits], axis=-1)
        w = jax.nn.softmax(all_logits, axis=-1)
        all_v = jnp.concatenate([V[:, :, :, None, :], nv], axis=3)
        out = jnp.einsum('bhln,bhlnd->bhld', w, all_v)
        out = out.transpose(0, 2, 1, 3).reshape(Bq, Lq, Dm)
        return out @ Wo.T + bo

    def _L0_ffn_ref(x, w1, b1, w2, b2):
        import jax, jax.numpy as jnp
        import numpy as np
        B, S, D = (4, 1024, 512)
        N_EXPERTS, EXPERT_SIZE = (16, 128)
        WIDTH = N_EXPERTS * EXPERT_SIZE
        h = jax.nn.relu(jnp.einsum('bsd,dw->bsw', x, w1) + b1)
        return jnp.einsum('bsw,wd->bsd', h, w2) + b2
    x = _layernorm(x + _L0_attn_ref(x, L0_attn_W_qkv, L0_attn_b_qkv), axis=-1)
    x = _layernorm(x + _L0_xattn_ref(x, ctx_1024, ctx_1024, L0_xattn_Wq, L0_xattn_Wk, L0_xattn_Wv, L0_xattn_Wo, L0_xattn_bo, itok_Sx12_0_8189, mask_Sx12_bk0), axis=-1)
    x = _layernorm(x + _L0_ffn_ref(x, L0_ffn_w1, L0_ffn_b1, L0_ffn_w2, L0_ffn_b2), axis=-1)
    return x

_drawn_inputs = setup_inputs


def setup_inputs(seed=0):
    import zlib

    import numpy as np

    out = dict(_drawn_inputs(seed))
    spreads = {'L0_ffn_b1': (0.0, 0.1), 'L0_ffn_b2': (0.0, 0.1)}
    factors = {'L0_attn_W_qkv': 8.0, 'L0_attn_b_qkv': 58.064, 'L0_xattn_bo': 64.0}
    for name, (base, spread) in spreads.items():
        noise = np.random.default_rng([zlib.crc32(name.encode()), seed]).standard_normal(out[name].shape)
        drawn = base * np.exp(spread * noise) if base else spread * noise
        out[name] = jnp.asarray(drawn.astype(out[name].dtype))
    for name, factor in factors.items():
        out[name] = (out[name] * factor).astype(out[name].dtype)
    return out
```

```python
from contextlib import ExitStack

import numpy as np

import concourse.bass as bass
from concourse import mybir

F32 = mybir.dt.float32
I32 = mybir.dt.int32
U8 = mybir.dt.uint8
ALU = mybir.AluOpType
ACT = mybir.ActivationFunctionType
AX = mybir.AxisListType

P = 128
B = 8
T = 512
D = 512
H = 16
DH = D // H
TT = T // P
KC = D // P
NODES = 2 * T - 1
FLAT = 2 * T
NT = FLAT // P
LEVELS = 9
NN = 12
NG = 3
GN = NN // NG
WIDTH = 2048
WC = WIDTH // P
EPS = 1e-5
SCALE = float(DH) ** -0.5
HIDE = -1e30

RING = 3
I_KVT = 0
I_QKV = I_KVT + 2 * KC
I_TREE = I_QKV + 2 * KC + TT
I_S = I_TREE + 2 * NT
UNITS = TT * H
N1 = I_S + UNITS
T_LAG, PV_LAG = 2, 3

RING2 = 2
I_Q0 = 0
I_LOOP = 2 * TT
I_TAIL = 0
I_Q = 2 * TT
I_X2T = 4 * TT
N2 = 5 * TT
EXP_AFTER = (3, 6, 10, 14)
POOL_V_GROUPS = (2,)


def decoder_layer(nc, x, xT, ctxT, idx, mask, wqkvT, bqk, bv, wkT, wvT, wqT, woT, bo, w1, b1, w2, b2,
                  rope, node_scale, ident_in, out):
    outer = ExitStack()
    with outer:
        def alloc(stack):
            def sb(name, shape, dt=F32):
                return stack.enter_context(nc.sbuf_tensor(name, shape, dt))

            def sem(name):
                return stack.enter_context(nc.semaphore(name))
            return sb, sem

        sb, sem = alloc(outer)
        bank = [outer.enter_context(nc.psum_tensor(f"bank{i}", [P, 512], F32)) for i in range(8)]
        kflat = nc.dram_tensor("kflat", [B * FLAT, D], F32, kind="Internal").ap()
        vflat = nc.dram_tensor("vflat", [B * FLAT, D], F32, kind="Internal").ap()
        x1_dram = nc.dram_tensor("x1_dram", [B, T, D], F32, kind="Internal").ap()

        ident = sb("ident", [P, P])
        w1_sb = sb("w1_sb", [P, KC, WIDTH])
        wq_sb = sb("wq_sb", [P, KC, D])
        consts_loaded = sem("consts_loaded")
        mlp_weights_loaded = sem("mlp_weights_loaded")
        waits_passed = sem("waits_passed")

        def chunks(w):
            return w.rearrange("(c p) n -> p c n", p=P)

        def row(v):
            return v.rearrange("(a n) -> a n", a=1).to_broadcast((P, v.shape[0]))

        with ExitStack() as stack:
            sb, sem = alloc(stack)
            wqkv_sb = sb("wqkv_sb", [P, KC, 3 * D])
            wk_sb = sb("wk_sb", [P, KC, D])
            wv_sb = sb("wv_sb", [P, KC, D])
            rope_sb = sb("rope_sb", [P, 4, T])
            bqk_sb = sb("bqk_sb", [P, 2 * KC])
            bv_sb = sb("bv_sb", [P, D])
            scale_sb = sb("scale_sb", [P, NT])
            xT_sb = sb("xT_sb", [P, KC, T])
            ctxT_sb = sb("ctxT_sb", [P, KC, T])
            xb = sb("xb", [P, TT, D])
            kvT = sb("kvT", [P, 2 * KC, FLAT])
            kv_nat = sb("kv_nat", [P, 4, D])
            raw = sb("raw", [P, 2, T])
            shuf = sb("shuf", [P, 2, T])
            qkT = sb("qkT", [P, 2 * KC, T])
            v_sb = sb("v_sb", [P, TT, D])
            probs = sb("probs", [P, 3, T])
            probsT = sb("probsT", [P, 3, T])
            neg_max = sb("neg_max", [P, 4])
            row_sum = sb("row_sum", [P, 2, H])
            inv_sum = sb("inv_sum", [P, H])
            attn = sb("attn", [P, D])
            stats = sb("stats", [P, 6])
            mean_var = sb("mean_var", [P, 2])
            var_eps = sb("var_eps", [P, 1])
            rstd = sb("rstd", [P, 1])
            half = sb("half", [P, 1])
            x1_out = sb("x1_out", [P, 2, D])

            ctx_loaded, xT_loaded, x_loaded = sem("ctx_loaded"), sem("xT_loaded"), sem("x_loaded")
            work_ready, work_free = sem("work_ready"), sem("work_free")
            tree_level, xb_ready = sem("tree_level"), sem("xb_ready")
            rope_step, rope_done = sem("rope_step"), sem("rope_done")
            kv_stored = [sem(f"kv_stored{i}") for i in range(4)]
            x1_stored = [sem(f"x1_stored{i}") for i in range(2)]
            max_ready, pt_ready = sem("max_ready"), sem("pt_ready")
            pt_copied = [sem("pt_copied_by_act"), sem("pt_copied_by_dve")]
            attn_ready, inv_ready, attn_norm = sem("attn_ready"), sem("inv_ready"), sem("attn_norm")
            res_ready, ln_part, stats_ready = sem("res_ready"), sem("ln_part"), sem("stats_ready")
            rstd_part, rstd_ready, x1_ready = sem("rstd_part"), sem("rstd_ready"), sem("x1_ready")
            pad_ready, half_ready = sem("pad_ready"), sem("half_ready")
            S, PT, O = bank[0:3], bank[3:5], bank[5:7]
            CONSTS = 16 * 9

            def stand_alone(eng):
                eng.sem_inc(waits_passed, 1)

            def loaded_act(eng, b, item):
                eng.wait_ge(work_free, b * N1 + RING + item + 1)

            block = stack.enter_context(nc.Block())

            @block.sync
            def _(sp):
                def load_ctx(b):
                    sp.dma_start(ctxT_sb[:], ctxT[bass.ds(b, 1)].rearrange("a (c p) t -> p (a c) t", p=P))\
                        .then_inc(ctx_loaded, 16)

                def load_xT(b):
                    sp.dma_start(xT_sb[:], xT[bass.ds(b, 1)].rearrange("a (c p) t -> p (a c) t", p=P))\
                        .then_inc(xT_loaded, 16)

                def load_x(b):
                    sp.dma_start(xb[:], x[bass.ds(b, 1)].rearrange("a (c p) d -> p (a c) d", p=P))\
                        .then_inc(x_loaded, 16)

                load_ctx(0)
                sp.dma_start(wk_sb[:], chunks(wkT)).then_inc(consts_loaded, 16)
                sp.dma_start(wv_sb[:], chunks(wvT)).then_inc(consts_loaded, 16)
                load_xT(0)
                sp.dma_start(wqkv_sb[:], chunks(wqkvT)).then_inc(consts_loaded, 16)
                sp.dma_start(bqk_sb[:], bqk).then_inc(consts_loaded, 16)
                sp.dma_start(bv_sb[:], row(bv)).then_inc(consts_loaded, 16)
                sp.dma_start(rope_sb[:], rope.rearrange("a p t -> p a t")).then_inc(consts_loaded, 16)
                sp.dma_start(scale_sb[:], node_scale).then_inc(consts_loaded, 16)
                sp.dma_start(ident[:], ident_in).then_inc(consts_loaded, 16)
                sp.dma_start(wq_sb[:], chunks(wqT)).then_inc(consts_loaded, 16)
                load_x(0)
                sp.dma_start(w1_sb[:], chunks(w1)).then_inc(mlp_weights_loaded, 16)

                def stores(b):
                    for t in range(2 * NT):
                        loaded_act(sp, b, I_TREE + t)
                        flat = kflat if t < NT else vflat
                        sp.dma_start(flat[bass.ds(b * FLAT + (t % NT) * P, P), :], kv_nat[:, t % 4, :])\
                            .then_inc(kv_stored[t % 4], 16)

                def store_x1(b):
                    for qt in range(TT):
                        sp.wait_ge(x1_ready, b * TT + qt + 1)
                        sp.dma_start(x1_dram[bass.ds(b, 1), qt * P:(qt + 1) * P, :].rearrange("a p d -> p (a d)"),
                                     x1_out[:, qt % 2, :]).then_inc(x1_stored[qt % 2], 16)

                with sp.Fori(0, B - 1) as b:
                    stores(b)
                    sp.wait_ge(work_ready, b * N1 + I_TREE)
                    load_ctx(b + 1)
                    load_xT(b + 1)
                    store_x1(b)
                    load_x(b + 1)
                stores(B - 1)
                store_x1(B - 1)
                for s in kv_stored:
                    sp.wait_ge(s, 16 * B * 2 * NT // 4)
                for s in x1_stored:
                    sp.wait_ge(s, 16 * B * TT // 2)
                sp.wait_ge(mlp_weights_loaded, 16)

            @block.tensor
            def _(pe):
                pe.wait_ge(consts_loaded, CONSTS)

                def take(b, item):
                    pe.wait_ge(work_free, b * N1 + max(item + 1, RING))
                    return S[item % RING]

                with pe.Fori(0, B) as b:
                    pe.wait_ge(ctx_loaded, b * 16 + 16)
                    for i in range(2 * KC):
                        w, f = (wk_sb, wv_sb)[i // KC], i % KC
                        o = take(b, I_KVT + i)
                        for c in range(KC):
                            mm = pe.matmul(o[:], w[:, c, f * P:(f + 1) * P], ctxT_sb[:, c, :],
                                           start=c == 0, stop=c == KC - 1)
                        mm.then_inc(work_ready, 1)
                    pe.wait_ge(xT_loaded, b * 16 + 16)
                    for i in range(2 * KC):
                        o = take(b, I_QKV + i)
                        for c in range(KC):
                            mm = pe.matmul(o[:], wqkv_sb[:, c, i * P:(i + 1) * P], xT_sb[:, c, :],
                                           start=c == 0, stop=c == KC - 1)
                        mm.then_inc(work_ready, 1)
                    for t in range(TT):
                        o = take(b, I_QKV + 2 * KC + t)
                        for c in range(KC):
                            mm = pe.matmul(o[:], xT_sb[:, c, t * P:(t + 1) * P], wqkv_sb[:, c, 2 * D:3 * D],
                                           start=c == 0, stop=c == KC - 1)
                        mm.then_inc(work_ready, 1)
                    pe.wait_ge(tree_level, b * LEVELS + LEVELS)
                    pe.wait_ge(pad_ready, 1)
                    for t in range(2 * NT):
                        kv, n = t // NT, t % NT
                        o = take(b, I_TREE + t)
                        for f in range(KC):
                            mm = pe.transpose(o[:, f * P:(f + 1) * P], kvT[:, kv * KC + f, n * P:(n + 1) * P],
                                              ident[:])
                        mm.then_inc(work_ready, 1)
                    pe.wait_ge(rope_done, b * 2 * KC + 2 * KC)
                    for s in range(UNITS + PV_LAG):
                        if s < UNITS:
                            qt, h = s // H, s % H
                            r = slice((h % 4) * DH, (h % 4 + 1) * DH)
                            o = take(b, I_S + s)
                            pe.matmul(o[:], qkT[r, h // 4, qt * P:(qt + 1) * P], qkT[r, KC + h // 4, :],
                                      start=True, stop=True).then_inc(work_ready, 1)
                        u = s - T_LAG
                        if 0 <= u < UNITS:
                            loaded_act(pe, b, I_S + u)
                            pe.wait_ge(pt_copied[u % 2], b * (UNITS // 2) + u // 2)
                            for k in range(TT):
                                mm = pe.transpose(PT[u % 2][:, k * P:(k + 1) * P],
                                                  probs[:, u % 3, k * P:(k + 1) * P], ident[:])
                            mm.then_inc(pt_ready, 1)
                        u = s - PV_LAG
                        if 0 <= u < UNITS:
                            qt, h = u // H, u % H
                            if h == 0:
                                pe.wait_ge(attn_norm, b * TT + max(qt - 1, 0))
                            pe.wait_ge(pt_copied[u % 2], b * (UNITS // 2) + u // 2 + 1)
                            for k in range(TT):
                                mm = pe.matmul(O[qt % 2][:, h * DH:(h + 1) * DH], probsT[:, u % 3, k * P:(k + 1) * P],
                                               v_sb[:, k, h * DH:(h + 1) * DH], start=k == 0, stop=k == TT - 1)
                            if h == H - 1:
                                mm.then_inc(attn_ready, 1)

            @block.scalar
            def _(act):
                act.sem_inc(work_free, RING)
                act.wait_ge(consts_loaded, CONSTS)
                with act.Fori(0, B) as b:
                    for i in range(2 * KC):
                        act.wait_ge(work_ready, b * N1 + I_KVT + i + 1)
                        act.activation(kvT[:, i, 0:T], S[(I_KVT + i) % RING][:], ACT.Copy).then_inc(work_free, 1)
                    for i in range(2 * KC):
                        act.wait_ge(work_ready, b * N1 + I_QKV + i + 1)
                        act.wait_ge(rope_done, b * 2 * KC + max(i - 1, 0))
                        act.activation(raw[:, i % 2, :], S[(I_QKV + i) % RING][:], ACT.Identity,
                                       bias=bqk_sb[:, i:i + 1]).then_inc(work_free, 1)
                    for t in range(TT):
                        item = I_QKV + 2 * KC + t
                        act.wait_ge(work_ready, b * N1 + item + 1)
                        act.activation(v_sb[:, t, :], S[item % RING][:], ACT.Copy).then_inc(work_free, 1)
                    for t in range(2 * NT):
                        item = I_TREE + t
                        act.wait_ge(work_ready, b * N1 + item + 1)
                        act.wait_ge(kv_stored[t % 4], b * (16 * 2 * NT // 4) + 16 * (t // 4))
                        if t < NT:
                            act.activation(kv_nat[:, t % 4, :], S[item % RING][:], ACT.Copy,
                                           scale=scale_sb[:, t:t + 1]).then_inc(work_free, 1)
                        else:
                            act.activation(kv_nat[:, t % 4, :], S[item % RING][:], ACT.Copy)\
                                .then_inc(work_free, 1)
                    for s in range(UNITS + T_LAG):
                        u = s - T_LAG
                        if u >= 0 and u % 2 == 0:
                            act.wait_ge(pt_ready, b * UNITS + u + 1)
                            act.activation(probsT[:, u % 3, :], PT[0][:], ACT.Copy).then_inc(pt_copied[0], 1)
                        if s < UNITS:
                            qt, h = s // H, s % H
                            act.wait_ge(pt_ready, b * UNITS + max(s - 2, 0))
                            act.wait_ge(max_ready, b * UNITS + s + 1)
                            act.activation(probs[:, s % 3, :], S[(I_S + s) % RING][:], ACT.Exp,
                                           bias=neg_max[:, s % 4:s % 4 + 1],
                                           accum_out=row_sum[:, qt % 2, h:h + 1]).then_inc(work_free, 1)

            @block.vector
            def _(dve):
                dve.wait_ge(consts_loaded, CONSTS)
                swap = [i ^ 1 for i in range(32)]
                with dve.Fori(0, B) as b:
                    for i in range(2 * KC):
                        cos, sin = rope_sb[:, 2 * (i // KC), :], rope_sb[:, 2 * (i // KC) + 1, :]
                        loaded_act(dve, b, I_QKV + i)
                        dve.wait_ge(rope_done, b * 2 * KC + max(i - 1, 0))
                        stand_alone(dve)
                        sh = shuf[:, i % 2, :]
                        dve.stream_shuffle(sh, raw[:, i % 2, :], swap).then_inc(rope_step, 1)
                        dve.tensor_tensor(qkT[:, i, :], raw[:, i % 2, :], cos, ALU.mult).then_inc(rope_step, 1)
                        dve.wait_ge(rope_step, b * 6 * KC + 3 * i + 1)
                        dve.tensor_tensor(sh, sh, sin, ALU.mult).then_inc(rope_step, 1)
                        dve.wait_ge(rope_step, b * 6 * KC + 3 * i + 3)
                        dve.tensor_tensor(qkT[:, i, :], qkT[:, i, :], sh, ALU.add).then_inc(rope_done, 1)
                    for s in range(UNITS + 8):
                        if s < UNITS:
                            dve.wait_ge(work_ready, b * N1 + I_S + s + 1)
                            dve.tensor_reduce(neg_max[:, s % 4:s % 4 + 1], S[(I_S + s) % RING][:], AX.X, ALU.max,
                                              negate=True).then_inc(max_ready, 1)
                        u = s - T_LAG
                        if 0 <= u < UNITS and u % 2 == 1:
                            dve.wait_ge(pt_ready, b * UNITS + u + 1)
                            dve.tensor_copy(probsT[:, u % 3, :], PT[1][:]).then_inc(pt_copied[1], 1)
                        qt, at = s // H - 1, s % H
                        if qt >= 0 and at == 3:
                            n = b * TT + qt
                            loaded_act(dve, b, I_S + qt * H + H - 1)
                            dve.wait_ge(attn_norm, n)
                            dve.reciprocal(inv_sum[:], row_sum[:, qt % 2, :]).then_inc(inv_ready, 1)
                            dve.wait_ge(inv_ready, n + 1)
                            dve.wait_ge(attn_ready, n + 1)
                            dve.wait_ge(x1_ready, n)
                            dve.tensor_tensor(attn[:].rearrange("p (h d) -> p h d", h=H),
                                              O[qt % 2][:].rearrange("p (h d) -> p h d", h=H),
                                              inv_sum[:].unsqueeze(2).to_broadcast([P, H, DH]),
                                              ALU.mult).then_inc(attn_norm, 1)
                        if qt >= 0 and at == 5:
                            n = b * TT + qt
                            dve.wait_ge(res_ready, n + 1)
                            dve.bn_stats(stats[:], attn[:]).then_inc(ln_part, 1)
                            dve.wait_ge(ln_part, n + 1)
                            stand_alone(dve)
                            dve.bn_aggr(mean_var[:], stats[:]).then_inc(stats_ready, 1)
                        if qt >= 0 and at == 7:
                            n = b * TT + qt
                            dve.wait_ge(rstd_ready, n + 1)
                            dve.wait_ge(x1_stored[qt % 2], b * (16 * TT // 2) + 16 * (qt // 2))
                            dve.tensor_scalar(x1_out[:, qt % 2, :], attn[:], mean_var[:, 0:1], rstd[:],
                                              ALU.subtract, ALU.mult).then_inc(x1_ready, 1)

            @block.gpsimd
            def _(pool):
                pool.memset(kvT[:, :, FLAT - 1:FLAT], 0.0).then_inc(pad_ready, 1)
                pool.memset(half[:], -0.5).then_inc(half_ready, 1)
                pool.wait_ge(consts_loaded, CONSTS)
                pool.wait_ge(half_ready, 1)
                with pool.Fori(0, B) as b:
                    loaded_act(pool, b, I_KVT + 2 * KC - 1)
                    src, n = 0, T
                    for level in range(LEVELS):
                        if level:
                            pool.wait_ge(tree_level, b * LEVELS + level)
                        pool.tensor_tensor(kvT[:, :, src + n:src + n + n // 2], kvT[:, :, src:src + n:2],
                                           kvT[:, :, src + 1:src + n:2], ALU.add).then_inc(tree_level, 1)
                        src, n = src + n, n // 2
                    pool.wait_ge(x_loaded, b * 16 + 16)
                    for t in range(TT):
                        pool.tensor_tensor(xb[:, t, :], xb[:, t, :], bv_sb[:], ALU.add).then_inc(xb_ready, 1)
                    for qt in range(TT):
                        n = b * TT + qt
                        pool.wait_ge(xb_ready, n + 1)
                        pool.wait_ge(attn_norm, n + 1)
                        pool.tensor_tensor(attn[:], attn[:], xb[:, qt, :], ALU.add).then_inc(res_ready, 1)
                        pool.wait_ge(stats_ready, n + 1)
                        stand_alone(pool)
                        pool.tensor_scalar(var_eps[:], mean_var[:, 1:2], EPS, None, ALU.add).then_inc(rstd_part, 1)
                        pool.wait_ge(rstd_part, n + 1)
                        pool.tensor_tensor(rstd[:], var_eps[:], half[:], ALU.pow).then_inc(rstd_ready, 1)

        with ExitStack() as stack:
            sb, sem = alloc(stack)
            wo_sb = sb("wo_sb", [P, KC, D])
            w2_sb = sb("w2_sb", [P, WC, D])
            b1_sb = sb("b1_sb", [P, WC])
            bo_sb = sb("bo_sb", [P, D])
            b2_sb = sb("b2_sb", [P, D])
            idx_in = sb("idx_in", [P, TT, NN], I32)
            idx_f = sb("idx_f", [P, TT, NN])
            idx_t = sb("idx_t", [P, TT, NN])
            idx_rows = sb("idx_rows", [P, TT, NN], I32)
            mask_in = sb("mask_in", [P, TT, NN // 4], I32)
            hide = sb("hide", [P, TT, NN])
            k_buf = sb("k_buf", [P, NN, D])
            v_buf = sb("v_buf", [P, NN, D])
            k_self = sb("k_self", [P, D])
            v_self = sb("v_self", [P, D])
            q_sb = sb("q_sb", [P, TT, D])
            logits = sb("logits", [P, 2, NN + 1, H])
            top = sb("top", [P, 2, H])
            weights = sb("weights", [P, 2, NN + 1, H])
            total = sb("total", [P, H])
            o_sb = sb("o_sb", [P, TT, D])
            x1_in = sb("x1_in", [P, 2, D])
            x1_res = sb("x1_res", [P, TT, D])
            actT = sb("actT", [P, 2, KC, P])
            y2 = sb("y2", [P, 2, D])
            x2 = sb("x2", [P, TT, D])
            x2T = sb("x2T", [P, KC, T])
            hid = sb("hid", [P, 2, T])
            y3 = sb("y3", [P, TT, D])
            stats = sb("stats2", [P, 2, 6])
            mean_var = sb("mean_var2", [P, 2, 2])
            var_eps = sb("var_eps2", [P, 2])
            rstd = sb("rstd2", [P, 2])
            half = sb("half2", [P, 1])

            consts2 = sem("consts2")
            CONSTS2 = 16 * 5
            w2_loaded = sem("w2_loaded")
            idx_step, idx_ready = sem("idx_step"), sem("idx_ready")
            hide_ready, half_ready = sem("hide_ready"), sem("half_ready2")
            k_gathered = [sem(f"k_gathered{g}") for g in range(NG)]
            v_gathered = [sem(f"v_gathered{g}") for g in range(NG)]
            k_self_loaded, v_self_loaded = sem("k_self_loaded"), sem("v_self_loaded")
            k_mul, k_used = sem("k_mul"), sem("k_used")
            max_step, norm_step = sem("max_step"), sem("norm_step")
            shifted, exp_done, weights_ready = sem("shifted"), sem("exp_done"), sem("weights_ready")
            v_mul_dve, v_mul_pool = sem("v_mul_dve"), sem("v_mul_pool")
            v_part, v_sum = sem("v_part"), sem("v_sum")
            x1_loaded = [sem("x1_loaded0"), sem("x1_loaded1")]
            res_loaded = sem("res_loaded")
            work_ready, work_free = sem("work_ready2"), sem("work_free2")
            ln_add, ln_in, ln_part, ln_stats = sem("ln_add"), sem("ln_in"), sem("ln_part2"), sem("ln_stats")
            ln_eps, ln_rstd, ln_out = sem("ln_eps"), sem("ln_rstd"), sem("ln_out")
            h_psum, h_ready = sem("h_psum"), sem("h_ready")
            mlp_ready, mlp_copied = sem("mlp_ready"), sem("mlp_copied")
            out_stored = sem("out_stored")
            W, HB, ACC = bank[0:2], bank[2:4], bank[4:8]
            V_STEPS = 4

            def stand_alone(eng):
                eng.sem_inc(waits_passed, 1)

            def item_done(eng, k):
                eng.wait_ge(work_free, RING2 + k + 1)

            def q_item(b, lt):
                return I_Q0 + 2 * lt if isinstance(b, int) and b == 0 else (b - 1) * N2 + I_LOOP + I_Q + 2 * lt

            def loop_item(b, k):
                return b * N2 + I_LOOP + k

            block = stack.enter_context(nc.Block())

            @block.sync
            def _(sp):
                def load_x1(b, lt):
                    sp.dma_start(x1_in[:, lt % 2, :],
                                 x1_dram[bass.ds(b, 1), lt * P:(lt + 1) * P, :].rearrange("a p d -> p (a d)"))\
                        .then_inc(x1_loaded[lt % 2], 16)

                def load_self(b, lt):
                    n = b * TT + lt
                    sp.wait_ge(k_used, n * (NG + 1))
                    sp.dma_start(k_self[:], kflat[bass.ds(b * FLAT + lt * P, P), :]).then_inc(k_self_loaded, 16)

                def load_self_v(b, lt):
                    n = b * TT + lt
                    sp.wait_ge(v_sum, n * V_STEPS)
                    sp.dma_start(v_self[:], vflat[bass.ds(b * FLAT + lt * P, P), :]).then_inc(v_self_loaded, 16)

                def load_res(b):
                    sp.dma_start(x1_res[:], x1_dram[bass.ds(b, 1)].rearrange("a (c p) d -> p (a c) d", p=P))\
                        .then_inc(res_loaded, 16)

                sp.dma_start(idx_in[:], idx.rearrange("(c p) n -> p c n", p=P)).then_inc(consts2, 16)
                sp.dma_start(mask_in[:], mask.rearrange("(c p) n -> p c n", p=P)).then_inc(consts2, 16)
                load_x1(0, 0)
                load_x1(0, 1)
                sp.dma_start(wo_sb[:], chunks(woT)).then_inc(w2_loaded, 16)
                sp.dma_start(bo_sb[:], row(bo)).then_inc(consts2, 16)
                sp.dma_start(b1_sb[:], b1).then_inc(consts2, 16)
                sp.dma_start(b2_sb[:], row(b2)).then_inc(consts2, 16)
                for lt in range(2, TT):
                    sp.wait_ge(work_ready, q_item(0, lt - 2) + 1)
                    load_x1(0, lt)
                sp.dma_start(w2_sb[:], chunks(w2)).then_inc(w2_loaded, 16)
                load_res(0)
                for lt in range(TT):
                    load_self(0, lt)
                    load_self_v(0, lt)

                def sequence(b, more):
                    if more:
                        load_x1(b + 1, 0)
                        load_x1(b + 1, 1)
                        for lt in range(2, TT):
                            sp.wait_ge(work_ready, q_item(b + 1, lt - 2) + 1)
                            load_x1(b + 1, lt)
                        sp.wait_ge(ln_in, b * 2 * TT + TT)
                        load_res(b + 1)
                        for lt in range(TT):
                            load_self(b + 1, lt)
                            load_self_v(b + 1, lt)
                    for t in range(TT):
                        sp.wait_ge(ln_out, b * 2 * TT + TT + t + 1)
                        sp.dma_start(out[bass.ds(b, 1), t * P:(t + 1) * P, :].rearrange("a p d -> p (a d)"),
                                     y3[:, t, :]).then_inc(out_stored, 16)

                with sp.Fori(0, B - 1) as b:
                    sequence(b, True)
                sequence(B - 1, False)
                sp.wait_ge(out_stored, 16 * B * TT)

            @block.tensor
            def _(pe):
                def take(k):
                    pe.wait_ge(work_free, k + 1)

                def queries(b):
                    for lt in range(TT):
                        k = q_item(b, lt)
                        take(k)
                        pe.wait_ge(x1_loaded[lt % 2], b * (16 * TT // 2) + 16 * (lt // 2 + 1))
                        for f in range(KC):
                            mm = pe.transpose(W[0][:, f * P:(f + 1) * P], x1_in[:, lt % 2, f * P:(f + 1) * P], ident[:])
                        mm.then_inc(work_ready, 1)
                        take(k + 1)
                        item_done(pe, k)
                        for c in range(KC):
                            mm = pe.matmul(W[1][:], actT[:, lt % 2, c, :], wq_sb[:, c, :], start=c == 0, stop=c == KC - 1)
                        mm.then_inc(work_ready, 1)

                def sequence(b, more):
                    for lt in range(TT):
                        k = loop_item(b, I_TAIL + 2 * lt)
                        take(k)
                        pe.wait_ge(v_sum, b * TT * V_STEPS + (lt + 1) * V_STEPS)
                        for f in range(KC):
                            mm = pe.transpose(W[0][:, f * P:(f + 1) * P], o_sb[:, lt, f * P:(f + 1) * P], ident[:])
                        mm.then_inc(work_ready, 1)
                        take(k + 1)
                        item_done(pe, k)
                        for c in range(KC):
                            mm = pe.matmul(W[1][:], actT[:, lt % 2, c, :], wo_sb[:, c, :], start=c == 0, stop=c == KC - 1)
                        mm.then_inc(work_ready, 1)
                    if more:
                        queries(b + 1)
                    first = loop_item(b, I_X2T if more else I_Q)
                    for lt in range(TT):
                        take(first + lt)
                        pe.wait_ge(ln_out, b * 2 * TT + lt + 1)
                        for f in range(KC):
                            mm = pe.transpose(W[lt % 2][:, f * P:(f + 1) * P], x2[:, lt, f * P:(f + 1) * P], ident[:])
                        mm.then_inc(work_ready, 1)
                    item_done(pe, first + TT - 1)
                    for c in range(WC + 1):
                        if c < WC:
                            pe.wait_ge(h_ready, b * WC + max(c - 1, 0))
                            for k in range(KC):
                                mm = pe.matmul(HB[c % 2][:], w1_sb[:, k, c * P:(c + 1) * P], x2T[:, k, :],
                                               start=k == 0, stop=k == KC - 1)
                            mm.then_inc(h_psum, 1)
                        if c > 0:
                            if c == 1:
                                pe.wait_ge(mlp_copied, b * TT)
                            pe.wait_ge(h_ready, b * WC + c)
                            for t in range(TT):
                                mm = pe.matmul(ACC[t][:], hid[:, (c - 1) % 2, t * P:(t + 1) * P], w2_sb[:, c - 1, :],
                                               start=c == 1, stop=c == WC)
                    mm.then_inc(mlp_ready, 1)

                queries(0)
                pe.wait_ge(w2_loaded, 2 * 16)
                with pe.Fori(0, B - 1) as b:
                    sequence(b, True)
                sequence(B - 1, False)

            @block.scalar
            def _(act):
                act.sem_inc(work_free, RING2)
                act.wait_ge(consts2, CONSTS2)

                def queries(b):
                    for lt in range(TT):
                        k = q_item(b, lt)
                        act.wait_ge(work_ready, k + 1)
                        act.activation(actT[:, lt % 2].rearrange("p c t -> p (c t)"), W[0][:], ACT.Copy)\
                            .then_inc(work_free, 1)
                        act.wait_ge(work_ready, k + 2)
                        act.wait_ge(k_used, b * TT * (NG + 1))
                        act.activation(q_sb[:, lt, :], W[1][:], ACT.Copy, scale=SCALE).then_inc(work_free, 1)

                def exponentials(b, lt):
                    n = b * TT + lt
                    act.wait_ge(shifted, n + 1)
                    act.activation(weights[:, lt % 2].rearrange("p n h -> p (n h)"),
                                   logits[:, lt % 2].rearrange("p n h -> p (n h)"), ACT.Exp).then_inc(exp_done, 1)

                def sequence(b, more):
                    for lt in range(TT):
                        k = loop_item(b, I_TAIL + 2 * lt)
                        act.wait_ge(work_ready, k + 1)
                        act.activation(actT[:, lt % 2].rearrange("p c t -> p (c t)"), W[0][:], ACT.Copy)\
                            .then_inc(work_free, 1)
                        act.wait_ge(work_ready, k + 2)
                        act.wait_ge(ln_out, b * 2 * TT + max(lt - 1, 0))
                        act.activation(y2[:, lt % 2, :], W[1][:], ACT.Copy).then_inc(work_free, 1)
                    if more:
                        queries(b + 1)
                    first = loop_item(b, I_X2T if more else I_Q)
                    for lt in range(TT):
                        act.wait_ge(work_ready, first + lt + 1)
                        act.activation(x2T[:, :, lt * P:(lt + 1) * P], W[lt % 2][:].rearrange("p (c t) -> p c t", c=KC),
                                       ACT.Copy).then_inc(work_free, 1)
                    for c in range(WC):
                        act.wait_ge(h_psum, b * WC + c + 1)
                        act.activation(hid[:, c % 2, :], HB[c % 2][:], ACT.Relu, bias=b1_sb[:, c:c + 1])\
                            .then_inc(h_ready, 1)
                        if more and c in EXP_AFTER:
                            exponentials(b + 1, EXP_AFTER.index(c))
                    act.wait_ge(mlp_ready, b + 1)
                    act.wait_ge(out_stored, b * (16 * TT))
                    for t in range(TT):
                        act.activation(y3[:, t, :], ACC[t][:], ACT.Copy).then_inc(mlp_copied, 1)

                queries(0)
                for lt in range(TT):
                    exponentials(0, lt)
                with act.Fori(0, B - 1) as b:
                    sequence(b, True)
                sequence(B - 1, False)

            @block.vector
            def _(dve):
                def broadcast_heads(w, n):
                    return w.unsqueeze(3).to_broadcast([P, n, H, DH])

                def keys(b, lt):
                    n = b * TT + lt
                    if lt == 0:
                        q_k = q_item(b, TT - 1) + 1
                        dve.wait_ge(work_free, RING2 + q_k + 1)
                    q = q_sb[:, lt, :]

                    def multiply(g):
                        if g < NG:
                            dve.wait_ge(k_gathered[g], n * (16 * GN) + 16 * GN)
                            kk = k_buf[:, g * GN:(g + 1) * GN, :]
                            dve.tensor_tensor(kk, kk, q.unsqueeze(1).to_broadcast([P, GN, D]), ALU.mult)\
                                .then_inc(k_mul, 1)
                        else:
                            dve.wait_ge(k_self_loaded, n * 16 + 16)
                            dve.tensor_tensor(k_self[:], k_self[:], q, ALU.mult).then_inc(k_mul, 1)

                    def reduce(g):
                        dve.wait_ge(k_mul, n * (NG + 1) + g + 1)
                        lo, m = g * GN, GN if g < NG else 1
                        src = k_buf[:, lo:lo + m, :] if g < NG else k_self[:].unsqueeze(1)
                        dve.tensor_reduce(logits[:, lt % 2, lo:lo + m, :], src.rearrange("p n (h d) -> p n h d", h=H),
                                          AX.X, ALU.add).then_inc(k_used, 1)

                    multiply(0)
                    for g in range(1, NG + 1):
                        multiply(g)
                        reduce(g - 1)
                    reduce(NG)
                    lg = logits[:, lt % 2]
                    dve.wait_ge(k_used, n * (NG + 1) + NG + 1)
                    dve.tensor_tensor(lg[:, 0:NN, :], lg[:, 0:NN, :],
                                      hide[:, lt, :].unsqueeze(2).to_broadcast([P, NN, H]), ALU.add).then_inc(max_step, 1)
                    dve.wait_ge(max_step, n * 2 + 1)
                    dve.tensor_reduce(top[:, lt % 2, :], lg.rearrange("p n h -> p h n"), AX.X, ALU.max).then_inc(max_step, 1)
                    dve.wait_ge(max_step, n * 2 + 2)
                    dve.tensor_tensor(lg, lg, top[:, lt % 2, :].unsqueeze(1).to_broadcast([P, NN + 1, H]),
                                      ALU.subtract).then_inc(shifted, 1)

                def normalise(b, lt):
                    n = b * TT + lt
                    wt = weights[:, lt % 2]
                    dve.wait_ge(exp_done, n + 1)
                    dve.tensor_reduce(total[:], wt.rearrange("p n h -> p h n"), AX.X, ALU.add).then_inc(norm_step, 1)
                    dve.wait_ge(norm_step, n * 2 + 1)
                    dve.reciprocal(total[:], total[:]).then_inc(norm_step, 1)
                    dve.wait_ge(norm_step, n * 2 + 2)
                    dve.tensor_tensor(wt, wt, total[:].unsqueeze(1).to_broadcast([P, NN + 1, H]), ALU.mult)\
                        .then_inc(weights_ready, 1)

                def values(b, lt):
                    n = b * TT + lt
                    wt = weights[:, lt % 2]
                    dve.wait_ge(weights_ready, n + 1)
                    for g in range(NG):
                        if g in POOL_V_GROUPS:
                            continue
                        dve.wait_ge(v_gathered[g], n * (16 * GN) + 16 * GN)
                        vv = v_buf[:, g * GN:(g + 1) * GN, :].rearrange("p n (h d) -> p n h d", h=H)
                        dve.tensor_tensor(vv, vv, broadcast_heads(wt[:, g * GN:(g + 1) * GN, :], GN), ALU.mult)\
                            .then_inc(v_mul_dve, 1)
                    dve.wait_ge(v_self_loaded, n * 16 + 16)
                    vs = v_self[:].rearrange("p (h d) -> p h d", h=H)
                    dve.tensor_tensor(vs, vs, wt[:, NN, :].unsqueeze(2).to_broadcast([P, H, DH]), ALU.mult)\
                        .then_inc(v_mul_dve, 1)
                    dve.wait_ge(v_mul_dve, (n + 1) * (NG + 1 - len(POOL_V_GROUPS)))
                    a, c, e = (v_buf[:, g * GN:(g + 1) * GN, :] for g in range(NG))
                    dve.tensor_tensor(a, a, c, ALU.add).then_inc(v_sum, 1)
                    dve.wait_ge(v_mul_pool, (n + 1) * len(POOL_V_GROUPS))
                    dve.wait_ge(v_sum, n * V_STEPS + 1)
                    dve.tensor_tensor(a, a, e, ALU.add).then_inc(v_sum, 1)
                    dve.wait_ge(v_sum, n * V_STEPS + 2)
                    dve.tensor_tensor(a[:, 0:2, :], a[:, 0:2, :], a[:, 2:4, :], ALU.add).then_inc(v_part, 1)
                    dve.wait_ge(v_part, n * 2 + 1)
                    dve.tensor_tensor(v_buf[:, 0, :], v_buf[:, 0, :], v_buf[:, 1, :], ALU.add).then_inc(v_part, 1)
                    dve.wait_ge(v_part, n * 2 + 2)
                    dve.tensor_tensor(o_sb[:, lt, :], v_buf[:, 0, :], v_self[:], ALU.add).then_inc(v_sum, 2)

                def attention(b):
                    keys(b, 0)
                    for lt in range(TT):
                        if lt + 1 < TT:
                            keys(b, lt + 1)
                        normalise(b, lt)
                        values(b, lt)

                def norm_stats(j, y):
                    dve.wait_ge(ln_in, j + 1)
                    dve.bn_stats(stats[:, 0, :], y).then_inc(ln_part, 1)
                    dve.wait_ge(ln_part, j + 1)
                    dve.wait_ge(ln_out, j)
                    stand_alone(dve)
                    dve.bn_aggr(mean_var[:, 0, :], stats[:, 0, :]).then_inc(ln_stats, 1)

                def norm_apply(j, dst, y):
                    dve.wait_ge(ln_rstd, j + 1)
                    dve.tensor_scalar(dst, y, mean_var[:, 0, 0:1], rstd[:, 0:1], ALU.subtract, ALU.mult)\
                        .then_inc(ln_out, 1)

                dve.wait_ge(consts2, CONSTS2)
                dve.tensor_copy(idx_f[:], idx_in[:]).then_inc(idx_step, 1)
                dve.wait_ge(idx_step, 1)
                dve.tensor_scalar(idx_t[:], idx_f[:], 0.0, float(NODES), ALU.is_lt, ALU.mult).then_inc(idx_step, 1)
                dve.wait_ge(idx_step, 2)
                dve.tensor_tensor(idx_f[:], idx_f[:], idx_t[:], ALU.add).then_inc(idx_step, 1)
                dve.wait_ge(idx_step, 3)
                dve.tensor_scalar(idx_f[:], idx_f[:], 0.0, float(NODES - 1), ALU.max, ALU.min).then_inc(idx_step, 1)
                dve.tensor_scalar(hide[:], mask_in[:].bitcast(U8), HIDE, None, ALU.mult).then_inc(hide_ready, 1)
                dve.wait_ge(hide_ready, 1)
                attention(0)

                def sequence(b, more):
                    for lt in range(TT):
                        j = b * 2 * TT + lt
                        norm_stats(j, y2[:, lt % 2, :])
                        norm_apply(j, x2[:, lt, :], y2[:, lt % 2, :])
                    if more:
                        attention(b + 1)
                    for t in range(TT):
                        j = b * 2 * TT + TT + t
                        norm_stats(j, y3[:, t, :])
                        norm_apply(j, y3[:, t, :], y3[:, t, :])

                with dve.Fori(0, B - 1) as b:
                    sequence(b, True)
                sequence(B - 1, False)

            @block.gpsimd
            def _(pool):
                def gather(dst, flat, lt, i, s):
                    stand_alone(pool)
                    pool.indirect_dma_start(dst, None, flat,
                                            bass.IndirectOffsetOnAxis(idx_rows[:, lt, i:i + 1], 0)).then_inc(s, 16)

                def gather_keys(b, lt):
                    n = b * TT + lt
                    pool.wait_ge(k_used, n * (NG + 1))
                    for g in range(NG):
                        for i in range(g * GN, (g + 1) * GN):
                            gather(k_buf[:, i, :], kflat, lt, i, k_gathered[g])

                def gather_values(b, lt):
                    n = b * TT + lt
                    pool.wait_ge(v_sum, n * V_STEPS)
                    for g in range(NG):
                        for i in range(g * GN, (g + 1) * GN):
                            gather(v_buf[:, i, :], vflat, lt, i, v_gathered[g])

                def rows(b):
                    if not (isinstance(b, int) and b == 0):
                        for s in k_gathered + v_gathered:
                            pool.wait_ge(s, b * (TT * 16 * GN))
                        stand_alone(pool)
                        pool.tensor_scalar(idx_f[:], idx_f[:], float(FLAT), None, ALU.add).then_inc(idx_step, 1)
                        pool.wait_ge(idx_step, b + 4)
                    stand_alone(pool)
                    pool.tensor_copy(idx_rows[:], idx_f[:]).then_inc(idx_ready, 1)
                    pool.wait_ge(idx_ready, b + 1)

                def weight_values(b, lt):
                    n = b * TT + lt
                    pool.wait_ge(weights_ready, n + 1)
                    for g in POOL_V_GROUPS:
                        pool.wait_ge(v_gathered[g], n * (16 * GN) + 16 * GN)
                        vv = v_buf[:, g * GN:(g + 1) * GN, :].rearrange("p n (h d) -> p n h d", h=H)
                        w = weights[:, lt % 2, g * GN:(g + 1) * GN, :].unsqueeze(3).to_broadcast([P, GN, H, DH])
                        pool.tensor_tensor(vv, vv, w, ALU.mult).then_inc(v_mul_pool, 1)

                def first_gathers(b):
                    rows(b)
                    gather_keys(b, 0)
                    gather_values(b, 0)

                def attention(b):
                    for lt in range(TT):
                        if lt + 1 < TT:
                            gather_keys(b, lt + 1)
                        weight_values(b, lt)
                        if lt + 1 < TT:
                            gather_values(b, lt + 1)

                def norm(j, y, res, bias, ready, value):
                    pool.wait_ge(ready, value)
                    pool.tensor_tensor(y, y, res, ALU.add).then_inc(ln_add, 1)
                    pool.wait_ge(ln_add, j + 1)
                    pool.tensor_tensor(y, y, bias, ALU.add).then_inc(ln_in, 1)
                    pool.wait_ge(ln_stats, j + 1)
                    stand_alone(pool)
                    pool.tensor_scalar(var_eps[:, 0:1], mean_var[:, 0, 1:2], EPS, None, ALU.add).then_inc(ln_eps, 1)
                    pool.wait_ge(ln_eps, j + 1)
                    pool.tensor_tensor(rstd[:, 0:1], var_eps[:, 0:1], half[:], ALU.pow).then_inc(ln_rstd, 1)

                pool.memset(half[:], -0.5).then_inc(half_ready, 1)
                pool.wait_ge(half_ready, 1)
                pool.wait_ge(consts2, CONSTS2)
                pool.wait_ge(idx_step, 4)
                first_gathers(0)
                attention(0)

                def sequence(b, more):
                    if more:
                        first_gathers(b + 1)
                    pool.wait_ge(res_loaded, b * 16 + 16)
                    for lt in range(TT):
                        k = loop_item(b, I_TAIL + 2 * lt + 1)
                        norm(b * 2 * TT + lt, y2[:, lt % 2, :], x1_res[:, lt, :], bo_sb[:],
                             work_free, RING2 + k + 1)
                    if more:
                        attention(b + 1)
                    for t in range(TT):
                        norm(b * 2 * TT + TT + t, y3[:, t, :], x2[:, t, :], b2_sb[:], mlp_copied, b * TT + t + 1)

                with pool.Fori(0, B - 1) as b:
                    sequence(b, True)
                sequence(B - 1, False)


def rope_tables():
    freq = np.float32(1.0) / np.float32(10000.0) ** (np.arange(0, DH, 2, dtype=np.float32) / np.float32(DH))
    ang = (np.arange(T, dtype=np.float32)[:, None] * freq[None, :]).astype(np.float64)
    d = np.arange(P) % DH
    cos, sin = np.cos(ang)[:, d // 2].T, np.sin(ang)[:, d // 2].T * np.where(d % 2 == 0, -1.0, 1.0)[:, None]
    return np.stack([cos * SCALE, sin * SCALE, cos, sin]).astype(np.float32)


def node_scales():
    s, at, n = np.ones(FLAT, np.float32), T, T // 2
    for level in range(1, LEVELS + 1):
        s[at:at + n] = 0.5 ** level
        at, n = at + n, n // 2
    return np.ascontiguousarray(s.reshape(NT, P).T)


def kernel(x, ctx_1024, itok_Sx12_0_8189, mask_Sx12_bk0, L0_attn_W_qkv, L0_attn_b_qkv, L0_xattn_Wq, L0_xattn_Wk,
           L0_xattn_Wv, L0_xattn_Wo, L0_xattn_bo, L0_ffn_w1, L0_ffn_b1, L0_ffn_w2, L0_ffn_b2):
    import concourse.bacc as bacc
    from concourse.bass_utils import run_bass_kernel_spmd

    x, ctx = np.asarray(x), np.asarray(ctx_1024)
    b_qkv = np.asarray(L0_attn_b_qkv)
    arrays = {
        "x": x, "xT": x.transpose(0, 2, 1), "ctxT": ctx.transpose(0, 2, 1),
        "idx": np.asarray(itok_Sx12_0_8189), "mask": np.ascontiguousarray(mask_Sx12_bk0).view(np.int32),
        "wqkvT": np.asarray(L0_attn_W_qkv).T, "bqk": b_qkv[:2 * D].reshape(2 * KC, P).T, "bv": b_qkv[2 * D:],
        "wkT": np.asarray(L0_xattn_Wk).T, "wvT": np.asarray(L0_xattn_Wv).T, "wqT": np.asarray(L0_xattn_Wq).T,
        "woT": np.asarray(L0_xattn_Wo).T, "bo": np.asarray(L0_xattn_bo),
        "w1": np.asarray(L0_ffn_w1), "b1": np.asarray(L0_ffn_b1).reshape(WC, P).T,
        "w2": np.asarray(L0_ffn_w2), "b2": np.asarray(L0_ffn_b2),
        "rope": rope_tables(), "node_scale": node_scales(), "ident_in": np.eye(P, dtype=np.float32),
    }
    arrays = {f"in_{k}": np.ascontiguousarray(v) for k, v in arrays.items()}
    nc = bacc.Bacc("TRN2", target_bir_lowering=False, num_devices=1)
    args = [nc.dram_tensor(k, v.shape, mybir.dt.from_np(v.dtype), kind="ExternalInput").ap() for k, v in arrays.items()]
    out = nc.dram_tensor("out", (B, T, D), F32, kind="ExternalOutput").ap()
    decoder_layer(nc, *args, out)
    r = run_bass_kernel_spmd(nc, [arrays], core_ids=[0])
    return r.results[0]["out"]
```

```python
from contextlib import ExitStack

import numpy as np

import concourse.bass as bass
from concourse import mybir

F32 = mybir.dt.float32
F16 = mybir.dt.float16
I32 = mybir.dt.int32
U8 = mybir.dt.uint8
ALU = mybir.AluOpType
ACT = mybir.ActivationFunctionType
AX = mybir.AxisListType

P = 128
B = 8
T = 512
D = 512
H = 16
DH = D // H
TT = T // P
KC = D // P
NODES = 2 * T - 1
FLAT = 2 * T
NT = FLAT // P
LEVELS = 9
NN = 12
GN = 2
NG = NN // GN
SLOTS = 8
WIDTH = 2048
WC = WIDTH // P
EPS = 1e-5
SCALE = float(DH) ** -0.5
START = 1
HIDE = -1e30

Q_UP, K_UP = 64.0, 16.0
ROW_SCALE = 4096.0
ONES = DH
VW = 64
M_ROW = 3 * DH
KS = M_ROW + 2

RING = 3
I_KVT = 0
I_QK = I_KVT + 2 * KC
I_V = I_QK + 2 * KC
I_TREE = I_V + TT
I_E = I_TREE + 2 * NT
UNITS = TT * H
N1 = I_E + UNITS
GROUP = UNITS // 4
M_LAG = GROUP + 2
E_LAG = GROUP + 5
PV_LAG = 2
PAIR = 2 * TT
O_COPY_LAG = E_LAG + PAIR - 1 + PV_LAG + 1
O_TURN_LAG = O_COPY_LAG + 1
PAIRS = UNITS // PAIR
STEPS = UNITS - PAIR + O_TURN_LAG + 1
MISC = 4 + PAIRS

RING2 = 2
I_LOOP = 2 * TT
I_TAIL = 0
I_Q = 2 * TT
I_X2T = 4 * TT
N2 = 5 * TT
EXP_AFTER = (3, 6, 10, 14)
POOL_V_GROUPS = (4, 5)
DVE_V_GROUPS = tuple(g for g in range(NG) if g not in POOL_V_GROUPS)


def misc_item(slot):
    if slot >= M_LAG and (slot - M_LAG) % GROUP == 0 and (slot - M_LAG) // GROUP < 4:
        return "max", (slot - M_LAG) // GROUP
    if slot >= O_TURN_LAG and (slot - O_TURN_LAG) % PAIR == 0 and (slot - O_TURN_LAG) // PAIR < PAIRS:
        return "out", (slot - O_TURN_LAG) // PAIR
    return None


MISC_SLOTS = [s for s in range(STEPS) if misc_item(s)]
MISC_OF_MAX = [MISC_SLOTS.index(M_LAG + g * GROUP) for g in range(4)]


def head_of(unit):
    return 4 * (unit % GROUP // TT) + unit // GROUP


def decoder_layer(nc, x, xT, ctxT, idx, mask, wqkvT, bqk, bv, wkT, wvT, wqT, woT, bo, w1, b1, w2, b2,
                  rope, node_scale, ident_in, out):
    outer = ExitStack()
    with outer:
        def alloc(stack):
            sems = []

            def sb(name, shape, dt=F32):
                return stack.enter_context(nc.sbuf_tensor(name, shape, dt))

            def sem(name):
                sems.append(stack.enter_context(nc.semaphore(name)))
                return sems[-1]
            return sb, sem, sems

        sb, sem, _ = alloc(outer)
        bank = [outer.enter_context(nc.psum_tensor(f"bank{i}", [P, 512], F32)) for i in range(8)]
        kv_flat = nc.dram_tensor("kv_flat", [B * FLAT, 2 * D], F32, kind="Internal").ap()
        x1_dram = nc.dram_tensor("x1_dram", [B, T, D], F32, kind="Internal").ap()

        ident = sb("ident", [P, P])
        waits_passed = sem("waits_passed")

        def stand_alone(eng):
            eng.sem_inc(waits_passed, 1)

        def chunks(w):
            return w.rearrange("(c p) n -> p c n", p=P)

        def row(v):
            return v.rearrange("(a n) -> a n", a=1).to_broadcast((P, v.shape[0]))

        with ExitStack() as stack:
            sb, sem, sems = alloc(stack)
            wqkv_sb = sb("wqkv_sb", [P, KC, 3 * D])
            wk_sb = sb("wk_sb", [P, KC, D])
            wv_sb = sb("wv_sb", [P, KC, D])
            rope_sb = sb("rope_sb", [P, 4, T])
            bqk_sb = sb("bqk_sb", [P, 2 * KC])
            bv_sb = sb("bv_sb", [P, D])
            scale_sb = sb("scale_sb", [P, NT])
            xT_sb = sb("xT_sb", [P, KC, T])
            ctxT_sb = sb("ctxT_sb", [P, KC, T])
            xb = sb("xb", [P, TT, D])
            kvT = sb("kvT", [P, 2 * KC, FLAT])
            kv_nat = sb("kv_nat", [P, 2, D])
            raw = sb("raw", [P, 2, T])
            shuf = sb("shuf", [P, 2, T])
            rot = sb("rot", [P, 2, T])
            hi = sb("hi", [P, 2, KC, T], F16)
            lo = sb("lo", [P, 2, KC, T], F16)
            q_stack = sb("q_stack", [KS, H, T], F16)
            k_stack = sb("k_stack", [KS, H, T], F16)
            v_sb = sb("v_sb", [P, TT, H, VW])
            probsT = sb("probsT", [P, 4, T])
            neg_max = sb("neg_max", [P, 2, GROUP])
            max_hi = sb("max_hi", [GROUP, P], F16)
            max_lo = sb("max_lo", [GROUP, P], F16)
            oT = sb("oT", [P, T])
            inv_sum = sb("inv_sum", [P, TT, 2])
            attn = sb("attn", [P, TT, D])
            stats = sb("stats", [P, 2, 6])
            mean_var = sb("mean_var", [P, 2, 2])
            var_eps = sb("var_eps", [P, 1])
            rstd = sb("rstd", [P, 2])
            half = sb("half", [P, 1])

            consts_loaded = sem("consts_loaded")
            ctx_loaded, xT_loaded, x_loaded = sem("ctx_loaded"), sem("xT_loaded"), sem("x_loaded")
            work_ready, work_free = sem("work_ready"), sem("work_free")
            tree_level, xb_ready = sem("tree_level"), sem("xb_ready")
            rope_step, rot_done, hi_done, lo_done = sem("rope_step"), sem("rot_done"), sem("hi_done"), sem("lo_done")
            stacked = sem("stacked")
            kv_stored = [sem(f"kv_stored{i}") for i in range(2)]
            x1_stored = sem("x1_stored")
            rows_scored, max_done = sem("rows_scored"), sem("max_done")
            misc_ready, misc_free = sem("misc_ready"), sem("misc_free")
            max_hi_done, max_stacked = sem("max_hi_done"), sem("max_stacked")
            probs_used, pair_done, pair_copied = sem("probs_used"), sem("pair_done"), sem("pair_copied")
            inv_ready = sem("inv_ready")
            res_ready, ln_part, stats_ready = sem("res_ready"), sem("ln_part"), sem("stats_ready")
            rstd_part, rstd_ready, x1_ready = sem("rstd_part"), sem("rstd_ready"), sem("x1_ready")
            filled, pad_filled = sem("filled"), sem("pad_filled")
            ROWS, WORK, O, MB = bank[0:2], bank[2:5], bank[5:7], bank[7]
            CONSTS = 16 * 8
            FILLS = 3

            def item_copied(b, item):
                return START + b * N1 + RING + item + 1

            block = stack.enter_context(nc.Block())

            @block.sync
            def _(sp):
                for s in sems:
                    sp.sem_inc(s, START)

                def load_ctx(b):
                    sp.dma_start(ctxT_sb[:], ctxT[bass.ds(b, 1)].rearrange("a (c p) t -> p (a c) t", p=P))\
                        .then_inc(ctx_loaded, 16)

                def load_xT(b):
                    sp.dma_start(xT_sb[:], xT[bass.ds(b, 1)].rearrange("a (c p) t -> p (a c) t", p=P))\
                        .then_inc(xT_loaded, 16)

                def load_x(b):
                    sp.dma_start(xb[:], x[bass.ds(b, 1)].rearrange("a (c p) d -> p (a c) d", p=P))\
                        .then_inc(x_loaded, 16)

                load_ctx(0)
                sp.dma_start(wk_sb[:], chunks(wkT)).then_inc(consts_loaded, 16)
                sp.dma_start(wv_sb[:], chunks(wvT)).then_inc(consts_loaded, 16)
                load_xT(0)
                sp.dma_start(wqkv_sb[:], chunks(wqkvT)).then_inc(consts_loaded, 16)
                sp.dma_start(bqk_sb[:], bqk).then_inc(consts_loaded, 16)
                sp.dma_start(bv_sb[:], row(bv)).then_inc(consts_loaded, 16)
                sp.dma_start(rope_sb[:], rope.rearrange("a p t -> p a t")).then_inc(consts_loaded, 16)
                sp.dma_start(scale_sb[:], node_scale).then_inc(consts_loaded, 16)
                sp.dma_start(ident[:], ident_in).then_inc(consts_loaded, 16)
                load_x(0)

                def stack_heads(b, qk):
                    sp.wait_ge(lo_done, START + b * 2 * KC + (qk + 1) * KC)
                    sp.wait_ge(work_ready, START + b * N1)
                    parts = (hi, hi, lo) if qk == 0 else (hi, lo, hi)
                    dst = (q_stack, k_stack)[qk]
                    for g in range(4):
                        for i, part in enumerate(parts):
                            sp.dma_start(dst[i * DH:(i + 1) * DH, 4 * g:4 * g + 4, :],
                                         part[g * DH:(g + 1) * DH, qk, :, :]).then_inc(stacked, 16)

                def store_tree(b):
                    for t in range(2 * NT):
                        sp.wait_ge(work_free, item_copied(b, I_TREE + t))
                        kv, n = t // NT, t % NT
                        sp.dma_start(kv_flat[bass.ds(b * FLAT + n * P, P), kv * D:(kv + 1) * D], kv_nat[:, t % 2, :])\
                            .then_inc(kv_stored[t % 2], 16)

                def stack_max(b, g):
                    sp.wait_ge(misc_free, START + b * MISC + MISC_OF_MAX[g] + 1)
                    for r, part in enumerate((max_hi, max_lo)):
                        sp.dma_start(q_stack[M_ROW + r:M_ROW + r + 1, 4 * g:4 * g + 4, :]
                                     .rearrange("a h (q t) -> a (h q) t", q=TT),
                                     part[:]).then_inc(max_stacked, 16)

                def store_x1(b):
                    for t in range(TT):
                        sp.wait_ge(x1_ready, START + b * TT + t + 1)
                        sp.dma_start(x1_dram[bass.ds(b, 1), t * P:(t + 1) * P, :].rearrange("a p d -> p (a d)"),
                                     attn[:, t, :]).then_inc(x1_stored, 16)

                def sequence(b, more):
                    stack_heads(b, 0)
                    stack_heads(b, 1)
                    store_tree(b)
                    if more:
                        load_ctx(b + 1)
                        load_xT(b + 1)
                    for g in range(4):
                        stack_max(b, g)
                    store_x1(b)
                    if more:
                        load_x(b + 1)

                with sp.Fori(0, B - 1) as b:
                    sequence(b, True)
                sequence(B - 1, False)
                for s in kv_stored:
                    sp.wait_ge(s, START + 16 * B * 2 * NT // 2)
                sp.wait_ge(x1_stored, START + 16 * B * TT)

            @block.tensor
            def _(pe):
                pe.wait_ge(consts_loaded, START + CONSTS)
                pe.wait_ge(filled, START + FILLS)
                pe.wait_ge(pad_filled, START + 1)

                def take(b, item):
                    pe.wait_ge(work_free, START + b * N1 + max(item + 1, RING))
                    return WORK[item % RING]

                with pe.Fori(0, B) as b:
                    pe.wait_ge(ctx_loaded, START + b * 16 + 16)
                    for i in range(2 * KC):
                        w, f = (wk_sb, wv_sb)[i // KC], i % KC
                        o = take(b, I_KVT + i)
                        for c in range(KC):
                            mm = pe.matmul(o[:], w[:, c, f * P:(f + 1) * P], ctxT_sb[:, c, :],
                                           start=c == 0, stop=c == KC - 1)
                        mm.then_inc(work_ready, 1)
                    pe.wait_ge(xT_loaded, START + b * 16 + 16)
                    for i in range(2 * KC):
                        o = take(b, I_QK + i)
                        for c in range(KC):
                            mm = pe.matmul(o[:], wqkv_sb[:, c, i * P:(i + 1) * P], xT_sb[:, c, :],
                                           start=c == 0, stop=c == KC - 1)
                        mm.then_inc(work_ready, 1)
                    for t in range(TT):
                        o = take(b, I_V + t)
                        for c in range(KC):
                            mm = pe.matmul(o[:], xT_sb[:, c, t * P:(t + 1) * P], wqkv_sb[:, c, 2 * D:3 * D],
                                           start=c == 0, stop=c == KC - 1)
                        mm.then_inc(work_ready, 1)
                    pe.wait_ge(tree_level, START + b * LEVELS + LEVELS)
                    pe.wait_ge(stacked, START + (b + 1) * (2 * 4 * 3 * 16))
                    for s in range(STEPS):
                        if s < 2 * NT:
                            kv, n = s // NT, s % NT
                            o = take(b, I_TREE + s)
                            for f in range(KC):
                                mm = pe.transpose(o[:, f * P:(f + 1) * P], kvT[:, kv * KC + f, n * P:(n + 1) * P],
                                                  ident[:])
                            mm.then_inc(work_ready, 1)
                        if s < UNITS:
                            h, qt = s // TT, s % TT
                            pe.wait_ge(max_done, START + b * UNITS + max(s - 1, 0))
                            pe.matmul(ROWS[s % 2][:], q_stack[0:M_ROW, h, qt * P:(qt + 1) * P],
                                      k_stack[0:M_ROW, h, :], start=True, stop=True).then_inc(rows_scored, 1)
                        e = s - E_LAG
                        if 0 <= e < UNITS:
                            h, kt = e // TT, e % TT
                            if e % GROUP == 0:
                                pe.wait_ge(max_stacked, START + b * (4 * 32) + 32 * (e // GROUP + 1))
                            o = take(b, I_E + e)
                            pe.matmul(o[:], k_stack[:, h, kt * P:(kt + 1) * P], q_stack[:, h, :],
                                      start=True, stop=True).then_inc(work_ready, 1)
                        e = s - E_LAG - PV_LAG
                        if 0 <= e < UNITS:
                            kt, side, pair = e % TT, e // TT % 2, e // PAIR
                            if e % PAIR == 0:
                                pe.wait_ge(pair_copied, START + b * PAIRS + max(pair - 1, 0))
                            pe.wait_ge(work_free, item_copied(b, I_E + e))
                            mm = pe.matmul(O[pair % 2][side * VW:(side + 1) * VW, :], v_sb[:, kt, head_of(e), :],
                                           probsT[:, e % 4, :], start=kt == 0, stop=kt == TT - 1)
                            mm.then_inc(pair_done if e % PAIR == PAIR - 1 else probs_used, 1)
                        what = misc_item(s)
                        if what:
                            pe.wait_ge(misc_free, START + b * MISC + MISC_SLOTS.index(s))
                            if what[0] == "max":
                                pe.wait_ge(max_done, START + b * UNITS + (what[1] + 1) * GROUP)
                                pe.transpose(MB[0:GROUP, 0:P], neg_max[:, what[1] % 2, :], ident[:])\
                                    .then_inc(misc_ready, 1)
                            else:
                                pe.wait_ge(pair_copied, START + b * PAIRS + what[1] + 1)
                                for t in range(TT):
                                    mm = pe.transpose(MB[:, t * P:(t + 1) * P], oT[:, t * P:(t + 1) * P], ident[:])
                                mm.then_inc(misc_ready, 1)

            @block.scalar
            def _(act):
                act.sem_inc(work_free, RING)
                act.wait_ge(consts_loaded, START + CONSTS)
                with act.Fori(0, B) as b:
                    def item(i):
                        act.wait_ge(work_ready, START + b * N1 + i + 1)
                        return WORK[i % RING][:]

                    for i in range(2 * KC):
                        act.activation(kvT[:, i, 0:T], item(I_KVT + i), ACT.Copy).then_inc(work_free, 1)
                    for i in range(2 * KC):
                        act.wait_ge(rot_done, START + b * 2 * KC + max(i - 1, 0))
                        act.activation(raw[:, i % 2, :], item(I_QK + i), ACT.Identity,
                                       bias=bqk_sb[:, i:i + 1]).then_inc(work_free, 1)
                    for t in range(TT):
                        act.activation(v_sb[:, t, :, 0:DH], item(I_V + t).rearrange("p (h d) -> p h d", h=H),
                                       ACT.Copy).then_inc(work_free, 1)
                    for s in range(STEPS):
                        if s < 2 * NT:
                            src = item(I_TREE + s)
                            act.wait_ge(kv_stored[s % 2], START + b * (16 * 2 * NT // 2) + 16 * (s // 2))
                            if s < NT:
                                act.activation(kv_nat[:, s % 2, :], src, ACT.Copy, scale=scale_sb[:, s:s + 1])\
                                    .then_inc(work_free, 1)
                            else:
                                act.activation(kv_nat[:, s % 2, :], src, ACT.Copy).then_inc(work_free, 1)
                        e = s - E_LAG
                        if 0 <= e < UNITS:
                            src = item(I_E + e)
                            act.activation(probsT[:, e % 4, :], src, ACT.Exp, scale=1.0 / (Q_UP * K_UP))\
                                .then_inc(work_free, 1)
                        p = s - O_COPY_LAG
                        if p >= 0 and p % PAIR == 0 and p // PAIR < PAIRS:
                            p //= PAIR
                            act.wait_ge(pair_done, START + b * PAIRS + p + 1)
                            before = MISC_SLOTS.index(O_TURN_LAG + PAIR * (p - 1)) + 1 if p else 0
                            act.wait_ge(misc_ready, START + b * MISC + before)
                            act.activation(oT[:], O[p % 2][:], ACT.Copy).then_inc(pair_copied, 1)

            @block.vector
            def _(dve):
                dve.memset(v_sb[:], 0.0).then_inc(filled, 1)
                dve.wait_ge(filled, START + 1)
                dve.memset(v_sb[:, :, :, ONES:ONES + 1], 1.0).then_inc(filled, 1)
                dve.memset(k_stack[M_ROW:KS, :, :], ROW_SCALE).then_inc(filled, 1)
                dve.wait_ge(consts_loaded, START + CONSTS)
                swap = [i ^ 1 for i in range(32)]
                with dve.Fori(0, B) as b:
                    for i in range(2 * KC):
                        qk, c, n = i // KC, i % KC, b * 2 * KC + i
                        cos, sin = rope_sb[:, 2 * qk, :], rope_sb[:, 2 * qk + 1, :]
                        sh, ro, r = shuf[:, i % 2, :], rot[:, i % 2, :], raw[:, i % 2, :]
                        dve.wait_ge(work_free, item_copied(b, I_QK + i))
                        dve.wait_ge(rot_done, START + b * 2 * KC + max(i - 1, 0))
                        dve.wait_ge(lo_done, START + b * 2 * KC + max(i - 1, 0))
                        stand_alone(dve)
                        dve.stream_shuffle(sh, r, swap).then_inc(rope_step, 1)
                        dve.tensor_tensor(ro, r, cos, ALU.mult).then_inc(rope_step, 1)
                        dve.wait_ge(rope_step, START + b * 6 * KC + 3 * i + 1)
                        dve.tensor_tensor(sh, sh, sin, ALU.mult).then_inc(rope_step, 1)
                        dve.wait_ge(rope_step, START + b * 6 * KC + 3 * i + 3)
                        dve.tensor_tensor(ro, ro, sh, ALU.add).then_inc(rot_done, 1)
                        dve.wait_ge(rot_done, START + n + 1)
                        dve.wait_ge(stacked, START + b * (2 * 4 * 3 * 16))
                        dve.tensor_copy(hi[:, qk, c, :], ro).then_inc(hi_done, 1)
                        dve.wait_ge(hi_done, START + n + 1)
                        dve.tensor_tensor(lo[:, qk, c, :], ro, hi[:, qk, c, :], ALU.subtract).then_inc(lo_done, 1)
                    for s in range(STEPS):
                        if s < UNITS:
                            g, at = s // GROUP, s % GROUP
                            dve.wait_ge(rows_scored, START + b * UNITS + s + 1)
                            dve.tensor_reduce(neg_max[:, g % 2, at:at + 1], ROWS[s % 2][:], AX.X, ALU.max,
                                              negate=True).then_inc(max_done, 1)
                        what = misc_item(s)
                        if what and what[0] == "max":
                            n = b * 4 + what[1]
                            dve.wait_ge(misc_ready, START + b * MISC + MISC_SLOTS.index(s) + 1)
                            dve.wait_ge(max_stacked, START + n * 32)
                            dve.tensor_scalar(max_hi[:], MB[0:GROUP, 0:P], 1.0 / ROW_SCALE, None, ALU.mult)\
                                .then_inc(max_hi_done, 1)
                            dve.wait_ge(max_hi_done, START + n + 1)
                            dve.scalar_tensor_tensor(out=max_lo[:], in0=MB[0:GROUP, 0:P], scalar=1.0 / ROW_SCALE,
                                                     in1=max_hi[:], op0=ALU.mult, op1=ALU.subtract)\
                                .then_inc(misc_free, 1)
                        if what and what[0] == "out":
                            p = what[1]
                            n = b * PAIRS + p
                            dve.wait_ge(misc_ready, START + b * MISC + MISC_SLOTS.index(s) + 1)
                            pair = MB[:].rearrange("p (t s w) -> p t s w", t=TT, s=2)
                            dve.wait_ge(misc_free, START + b * MISC + MISC_SLOTS.index(s))
                            dve.reciprocal(inv_sum[:].unsqueeze(3), pair[:, :, :, ONES:ONES + 1])\
                                .then_inc(inv_ready, 1)
                            dve.wait_ge(inv_ready, START + n + 1)
                            dve.wait_ge(x1_stored, START + b * (16 * TT))
                            h = head_of(p * PAIR)
                            cols = attn[:].rearrange("p t (h d) -> p t h d", h=H)[:, :, h:h + 5:4, :]
                            dve.tensor_tensor(cols, pair[:, :, :, 0:DH],
                                              inv_sum[:].unsqueeze(3).to_broadcast([P, TT, 2, DH]),
                                              ALU.mult).then_inc(misc_free, 1)

                    def norm_stats(t):
                        n = b * TT + t
                        dve.wait_ge(res_ready, START + n + 1)
                        dve.bn_stats(stats[:, t % 2, :], attn[:, t, :]).then_inc(ln_part, 1)
                        dve.wait_ge(ln_part, START + n + 1)
                        dve.wait_ge(x1_ready, START + b * TT + max(t - 1, 0))
                        stand_alone(dve)
                        dve.bn_aggr(mean_var[:, t % 2, :], stats[:, t % 2, :]).then_inc(stats_ready, 1)

                    def norm_apply(t):
                        dve.wait_ge(rstd_ready, START + b * TT + t + 1)
                        dve.tensor_scalar(attn[:, t, :], attn[:, t, :], mean_var[:, t % 2, 0:1],
                                          rstd[:, t % 2:t % 2 + 1], ALU.subtract, ALU.mult).then_inc(x1_ready, 1)

                    norm_stats(0)
                    for t in range(TT):
                        if t + 1 < TT:
                            norm_stats(t + 1)
                        norm_apply(t)

            @block.gpsimd
            def _(pool):
                pool.memset(kvT[:, :, FLAT - 1:FLAT], 0.0).then_inc(pad_filled, 1)
                pool.memset(half[:], -0.5).then_inc(rstd_part, 1)
                pool.wait_ge(consts_loaded, START + CONSTS)
                pool.wait_ge(rstd_part, START + 1)
                with pool.Fori(0, B) as b:
                    pool.wait_ge(work_free, item_copied(b, I_KVT + 2 * KC - 1))
                    src, n = 0, T
                    for level in range(LEVELS):
                        if level:
                            pool.wait_ge(tree_level, START + b * LEVELS + level)
                        pool.tensor_tensor(kvT[:, :, src + n:src + n + n // 2], kvT[:, :, src:src + n:2],
                                           kvT[:, :, src + 1:src + n:2], ALU.add).then_inc(tree_level, 1)
                        src, n = src + n, n // 2
                    pool.wait_ge(x_loaded, START + b * 16 + 16)
                    for t in range(TT):
                        pool.tensor_tensor(xb[:, t, :], xb[:, t, :], bv_sb[:], ALU.add).then_inc(xb_ready, 1)

                    def add_residual(t):
                        pool.tensor_tensor(attn[:, t, :], attn[:, t, :], xb[:, t, :], ALU.add).then_inc(res_ready, 1)

                    def rstd_of(t):
                        n = b * TT + t
                        pool.wait_ge(stats_ready, START + n + 1)
                        pool.wait_ge(rstd_ready, START + n)
                        stand_alone(pool)
                        pool.tensor_scalar(var_eps[:], mean_var[:, t % 2, 1:2], EPS, None, ALU.add)\
                            .then_inc(rstd_part, 1)
                        pool.wait_ge(rstd_part, START + n + 2)
                        pool.tensor_tensor(rstd[:, t % 2:t % 2 + 1], var_eps[:], half[:], ALU.pow)\
                            .then_inc(rstd_ready, 1)

                    pool.wait_ge(xb_ready, START + b * TT + TT)
                    pool.wait_ge(misc_free, START + b * MISC + MISC)
                    add_residual(0)
                    for t in range(TT):
                        if t + 1 < TT:
                            add_residual(t + 1)
                        rstd_of(t)

        with ExitStack() as stack:
            sb, sem, sems = alloc(stack)
            w1_sb = sb("w1_sb", [P, KC, WIDTH])
            w2_sb = sb("w2_sb", [P, WC, D])
            wq_sb = sb("wq_sb", [P, KC, D])
            wo_sb = sb("wo_sb", [P, KC, D])
            b1_sb = sb("b1_sb", [P, WC])
            bo_sb = sb("bo_sb", [P, D])
            b2_sb = sb("b2_sb", [P, D])
            idx_in = sb("idx_in", [P, TT, NN], I32)
            idx_f = sb("idx_f", [P, TT, NN])
            idx_t = sb("idx_t", [P, TT, NN])
            idx_rows = sb("idx_rows", [P, TT, NN], I32)
            mask_in = sb("mask_in", [P, TT, NN // 4], I32)
            hide = sb("hide", [P, TT, NN])
            nb = sb("nb", [P, SLOTS, GN, 2 * D])
            own = sb("own", [P, 2 * D])
            q_sb = sb("q_sb", [P, TT, D])
            logits = sb("logits", [P, NN + 1, H])
            top = sb("top", [P, H])
            weights = sb("weights", [P, NN + 1, H])
            total = sb("total", [P, H])
            o_sb = sb("o_sb", [P, TT, D])
            x1_in = sb("x1_in", [P, D])
            x1_res = sb("x1_res", [P, D])
            actT = sb("actT", [P, KC, P])
            x2 = sb("x2", [P, TT, D])
            x2T = sb("x2T", [P, KC, T])
            hid = sb("hid", [P, 2, T])
            y3 = sb("y3", [P, 2, D])
            stats = sb("stats2", [P, 2, 6])
            mean_var = sb("mean_var2", [P, 2, 2])
            var_eps = sb("var_eps2", [P, 1])
            rstd = sb("rstd2", [P, 2])
            half = sb("half2", [P, 1])

            consts2, w_loaded = sem("consts2"), sem("w_loaded")
            CONSTS2 = 16 * 6
            WEIGHTS = 16 * 3
            idx_step, idx_ready, hide_ready = sem("idx_step"), sem("idx_ready"), sem("hide_ready")
            gathered = [sem(f"gathered{i}") for i in range(SLOTS)]
            own_loaded = sem("own_loaded")
            k_mul, k_sum = sem("k_mul"), sem("k_sum")
            max_step, shifted, exp_done = sem("max_step"), sem("shifted"), sem("exp_done")
            norm_step, weights_ready = sem("norm_step"), sem("weights_ready")
            v_mul_dve, v_mul_pool, v_pair, o_part = sem("v_mul_dve"), sem("v_mul_pool"), sem("v_pair"), sem("o_part")
            x1_loaded, res_loaded = sem("x1_loaded"), sem("res_loaded")
            work_ready, work_free = sem("work_ready2"), sem("work_free2")
            ln_add, ln_in, ln_part, ln_stats = sem("ln_add"), sem("ln_in"), sem("ln_part2"), sem("ln_stats")
            ln_eps, ln_rstd, ln_out = sem("ln_eps"), sem("ln_rstd"), sem("ln_out")
            h_psum, h_ready = sem("h_psum"), sem("h_ready")
            mlp_ready, mlp_copied = sem("mlp_ready"), sem("mlp_copied")
            out_stored = [sem("out_stored0"), sem("out_stored1")]
            WORK, HB, ACC = bank[0:2], bank[2:4], bank[4:8]

            def item_copied(k):
                return START + RING2 + k + 1

            def q_item(b, lt):
                return 2 * lt if isinstance(b, int) and b == 0 else (b - 1) * N2 + I_LOOP + I_Q + 2 * lt

            def loop_item(b, k):
                return b * N2 + I_LOOP + k

            def slot(lt, g):
                return (lt * NG + g) % SLOTS

            def fills(b, lt, g):
                return b * (TT * NG // SLOTS) + (lt * NG + g) // SLOTS + 1

            block = stack.enter_context(nc.Block())

            @block.sync
            def _(sp):
                for s in sems:
                    if s not in gathered:
                        sp.sem_inc(s, START)

                def load_x1(b, lt):
                    sp.dma_start(x1_in[:],
                                 x1_dram[bass.ds(b, 1), lt * P:(lt + 1) * P, :].rearrange("a p d -> p (a d)"))\
                        .then_inc(x1_loaded, 16)

                def load_own(b, lt):
                    if lt or not isinstance(b, int):
                        sp.wait_ge(o_part, START + b * (TT * (NG + 1)) + (lt - 1) * (NG + 1) + 1)
                    sp.dma_start(own[:], kv_flat[bass.ds(b * FLAT + lt * P, P), :]).then_inc(own_loaded, 16)

                def load_res(b, lt):
                    sp.wait_ge(ln_add, START + b * 2 * TT + lt)
                    stand_alone(sp)
                    sp.dma_start(x1_res[:],
                                 x1_dram[bass.ds(b, 1), lt * P:(lt + 1) * P, :].rearrange("a p d -> p (a d)"))\
                        .then_inc(res_loaded, 16)

                load_x1(0, 0)
                sp.dma_start(wq_sb[:], chunks(wqT)).then_inc(consts2, 16)
                sp.dma_start(idx_in[:], idx.rearrange("(c p) n -> p c n", p=P)).then_inc(consts2, 16)
                sp.dma_start(mask_in[:], mask.rearrange("(c p) n -> p c n", p=P)).then_inc(consts2, 16)
                sp.dma_start(bo_sb[:], row(bo)).then_inc(consts2, 16)
                sp.dma_start(b1_sb[:], b1).then_inc(consts2, 16)
                sp.dma_start(b2_sb[:], row(b2)).then_inc(consts2, 16)
                load_own(0, 0)

                def rest_x1(b):
                    for lt in range(1, TT):
                        sp.wait_ge(work_ready, START + q_item(b, lt - 1) + 1)
                        load_x1(b, lt)

                rest_x1(0)
                sp.dma_start(wo_sb[:], chunks(woT)).then_inc(w_loaded, 16)
                sp.dma_start(w1_sb[:], chunks(w1)).then_inc(w_loaded, 16)
                sp.dma_start(w2_sb[:], chunks(w2)).then_inc(w_loaded, 16)
                for lt in range(1, TT):
                    load_own(0, lt)
                load_res(0, 0)
                load_x1(1, 0)

                def sequence(b, more, last=False):
                    for lt in range(1, TT):
                        load_res(b, lt)
                    if more:
                        rest_x1(b + 1)
                        for lt in range(TT):
                            load_own(b + 1, lt)
                    for t in range(TT):
                        sp.wait_ge(ln_out, START + b * 2 * TT + TT + t + 1)
                        stand_alone(sp)
                        sp.dma_start(out[bass.ds(b, 1), t * P:(t + 1) * P, :].rearrange("a p d -> p (a d)"),
                                     y3[:, t % 2, :]).then_inc(out_stored[t % 2], 16)
                    if more:
                        load_res(b + 1, 0)
                    if more and not last:
                        load_x1(b + 2, 0)

                with sp.Fori(0, B - 2) as b:
                    sequence(b, True)
                sequence(B - 2, True, last=True)
                sequence(B - 1, False)
                for s in out_stored:
                    sp.wait_ge(s, START + 16 * B * TT // 2)

            @block.tensor
            def _(pe):
                def take(k):
                    pe.wait_ge(work_free, START + k + 1)

                def queries(b):
                    for lt in range(TT):
                        k = q_item(b, lt)
                        take(k)
                        pe.wait_ge(x1_loaded, START + b * (16 * TT) + 16 * (lt + 1))
                        for f in range(KC):
                            mm = pe.transpose(WORK[0][:, f * P:(f + 1) * P], x1_in[:, f * P:(f + 1) * P], ident[:])
                        mm.then_inc(work_ready, 1)
                        take(k + 1)
                        pe.wait_ge(work_free, item_copied(k))
                        for c in range(KC):
                            mm = pe.matmul(WORK[1][:], actT[:, c, :], wq_sb[:, c, :], start=c == 0, stop=c == KC - 1)
                        mm.then_inc(work_ready, 1)

                def sequence(b, more):
                    for lt in range(TT):
                        k = loop_item(b, I_TAIL + 2 * lt)
                        take(k)
                        pe.wait_ge(o_part, START + b * (TT * (NG + 1)) + (lt + 1) * (NG + 1))
                        for f in range(KC):
                            mm = pe.transpose(WORK[0][:, f * P:(f + 1) * P], o_sb[:, lt, f * P:(f + 1) * P], ident[:])
                        mm.then_inc(work_ready, 1)
                        take(k + 1)
                        pe.wait_ge(work_free, item_copied(k))
                        for c in range(KC):
                            mm = pe.matmul(WORK[1][:], actT[:, c, :], wo_sb[:, c, :], start=c == 0, stop=c == KC - 1)
                        mm.then_inc(work_ready, 1)
                    if more:
                        queries(b + 1)
                    first = loop_item(b, I_X2T if more else I_Q)
                    for lt in range(TT):
                        take(first + lt)
                        pe.wait_ge(ln_out, START + b * 2 * TT + lt + 1)
                        for f in range(KC):
                            mm = pe.transpose(WORK[lt % 2][:, f * P:(f + 1) * P], x2[:, lt, f * P:(f + 1) * P], ident[:])
                        mm.then_inc(work_ready, 1)
                    pe.wait_ge(work_free, item_copied(first + TT - 1))
                    for c in range(WC + 1):
                        if c < WC:
                            pe.wait_ge(h_ready, START + b * WC + max(c - 1, 0))
                            for k in range(KC):
                                mm = pe.matmul(HB[c % 2][:], w1_sb[:, k, c * P:(c + 1) * P], x2T[:, k, :],
                                               start=k == 0, stop=k == KC - 1)
                            mm.then_inc(h_psum, 1)
                        if c > 0:
                            if c == 1:
                                pe.wait_ge(mlp_copied, START + b * TT)
                            pe.wait_ge(h_ready, START + b * WC + c)
                            for t in range(TT):
                                mm = pe.matmul(ACC[t][:], hid[:, (c - 1) % 2, t * P:(t + 1) * P], w2_sb[:, c - 1, :],
                                               start=c == 1, stop=c == WC)
                    mm.then_inc(mlp_ready, 1)

                pe.wait_ge(consts2, START + CONSTS2)
                queries(0)
                pe.wait_ge(w_loaded, START + WEIGHTS)
                with pe.Fori(0, B - 1) as b:
                    sequence(b, True)
                sequence(B - 1, False)

            @block.scalar
            def _(act):
                act.sem_inc(work_free, RING2)
                act.wait_ge(consts2, START + CONSTS2)

                def transposed(k):
                    act.wait_ge(work_ready, START + k + 1)
                    act.activation(actT[:].rearrange("p c t -> p (c t)"), WORK[0][:], ACT.Copy).then_inc(work_free, 1)

                def queries(b):
                    for lt in range(TT):
                        k = q_item(b, lt)
                        transposed(k)
                        act.wait_ge(work_ready, START + k + 2)
                        act.wait_ge(k_sum, START + b * (TT * (NG + 1)))
                        act.activation(q_sb[:, lt, :], WORK[1][:], ACT.Copy, scale=SCALE).then_inc(work_free, 1)

                def exponentials(b, lt):
                    n = b * TT + lt
                    act.wait_ge(shifted, START + n + 1)
                    act.activation(weights[:].rearrange("p n h -> p (n h)"),
                                   logits[:].rearrange("p n h -> p (n h)"), ACT.Exp).then_inc(exp_done, 1)

                def sequence(b, more):
                    for lt in range(TT):
                        k = loop_item(b, I_TAIL + 2 * lt)
                        transposed(k)
                        act.wait_ge(work_ready, START + k + 2)
                        if lt == 0:
                            act.wait_ge(ln_in, START + b * 2 * TT)
                        act.activation(x2[:, lt, :], WORK[1][:], ACT.Copy).then_inc(work_free, 1)
                    if more:
                        queries(b + 1)
                    first = loop_item(b, I_X2T if more else I_Q)
                    for lt in range(TT):
                        act.wait_ge(work_ready, START + first + lt + 1)
                        act.activation(x2T[:, :, lt * P:(lt + 1) * P], WORK[lt % 2][:].rearrange("p (c t) -> p c t", c=KC),
                                       ACT.Copy).then_inc(work_free, 1)
                    for c in range(WC):
                        act.wait_ge(h_psum, START + b * WC + c + 1)
                        act.activation(hid[:, c % 2, :], HB[c % 2][:], ACT.Relu, bias=b1_sb[:, c:c + 1])\
                            .then_inc(h_ready, 1)
                        if more and c in EXP_AFTER:
                            exponentials(b + 1, EXP_AFTER.index(c))
                    act.wait_ge(mlp_ready, START + b + 1)
                    for t in range(TT):
                        act.wait_ge(out_stored[t % 2], START + b * (16 * TT // 2) + 16 * (t // 2))
                        act.activation(y3[:, t % 2, :], ACC[t][:], ACT.Copy).then_inc(mlp_copied, 1)

                queries(0)
                for lt in range(TT):
                    exponentials(0, lt)
                with act.Fori(0, B - 1) as b:
                    sequence(b, True)
                sequence(B - 1, False)

            @block.vector
            def _(dve):
                def keys(b, lt):
                    n = b * TT + lt
                    if lt == 0:
                        dve.wait_ge(work_free, item_copied(q_item(b, TT - 1) + 1))
                    q = q_sb[:, lt, :]

                    def multiply(g):
                        if g < NG:
                            dve.wait_ge(gathered[slot(lt, g)], (16 * GN) * fills(b, lt, g))
                            kk = nb[:, slot(lt, g), :, 0:D]
                            dve.tensor_tensor(kk, kk, q.unsqueeze(1).to_broadcast([P, GN, D]), ALU.mult)\
                                .then_inc(k_mul, 1)
                        else:
                            dve.wait_ge(own_loaded, START + n * 16 + 16)
                            dve.tensor_tensor(own[:, 0:D], own[:, 0:D], q, ALU.mult).then_inc(k_mul, 1)

                    def reduce(g):
                        dve.wait_ge(k_mul, START + n * (NG + 1) + g + 1)
                        if g < NG:
                            dve.tensor_reduce(logits[:, g * GN:(g + 1) * GN, :],
                                              nb[:, slot(lt, g), :, 0:D].rearrange("p n (h d) -> p n h d", h=H),
                                              AX.X, ALU.add).then_inc(k_sum, 1)
                        else:
                            dve.tensor_reduce(logits[:, NN, :], own[:, 0:D].rearrange("p (h d) -> p h d", h=H),
                                              AX.X, ALU.add).then_inc(k_sum, 1)

                    multiply(0)
                    for g in range(1, NG + 1):
                        multiply(g)
                        reduce(g - 1)
                    reduce(NG)
                    dve.wait_ge(k_sum, START + n * (NG + 1) + NG + 1)
                    dve.tensor_tensor(logits[:, 0:NN, :], logits[:, 0:NN, :],
                                      hide[:, lt, :].unsqueeze(2).to_broadcast([P, NN, H]), ALU.add)\
                        .then_inc(max_step, 1)
                    dve.wait_ge(max_step, START + n * 2 + 1)
                    dve.tensor_reduce(top[:], logits[:].rearrange("p n h -> p h n"), AX.X, ALU.max)\
                        .then_inc(max_step, 1)
                    dve.wait_ge(max_step, START + n * 2 + 2)
                    dve.tensor_tensor(logits[:], logits[:], top[:].unsqueeze(1).to_broadcast([P, NN + 1, H]),
                                      ALU.subtract).then_inc(shifted, 1)

                def normalise(b, lt):
                    n = b * TT + lt
                    dve.wait_ge(exp_done, START + n + 1)
                    dve.tensor_reduce(total[:], weights[:].rearrange("p n h -> p h n"), AX.X, ALU.add)\
                        .then_inc(norm_step, 1)
                    dve.wait_ge(norm_step, START + n * 2 + 1)
                    dve.reciprocal(total[:], total[:]).then_inc(norm_step, 1)
                    dve.wait_ge(norm_step, START + n * 2 + 2)
                    dve.tensor_tensor(weights[:], weights[:], total[:].unsqueeze(1).to_broadcast([P, NN + 1, H]),
                                      ALU.mult).then_inc(weights_ready, 1)

                def values(b, lt):
                    n = b * TT + lt
                    dve.wait_ge(weights_ready, START + n + 1)

                    def multiply(g):
                        dve.wait_ge(gathered[slot(lt, g)], (16 * GN) * fills(b, lt, g))
                        vv = nb[:, slot(lt, g), :, D:2 * D].rearrange("p n (h d) -> p n h d", h=H)
                        w = weights[:, g * GN:(g + 1) * GN, :].unsqueeze(3).to_broadcast([P, GN, H, DH])
                        dve.tensor_tensor(vv, vv, w, ALU.mult).then_inc(v_mul_dve, 1)

                    def pair(g):
                        if g in POOL_V_GROUPS:
                            dve.wait_ge(v_mul_pool, START + n * len(POOL_V_GROUPS) + POOL_V_GROUPS.index(g) + 1)
                        else:
                            dve.wait_ge(v_mul_dve, START + n * len(DVE_V_GROUPS) + DVE_V_GROUPS.index(g) + 1)
                        v = nb[:, slot(lt, g), :, D:2 * D]
                        dve.tensor_tensor(v[:, 0, :], v[:, 0, :], v[:, 1, :], ALU.add).then_inc(v_pair, 1)

                    def accumulate(g):
                        dve.wait_ge(v_pair, START + n * NG + g + 1)
                        dve.wait_ge(o_part, START + n * (NG + 1) + g + 1)
                        v = nb[:, slot(lt, g), 0, D:2 * D]
                        dve.tensor_tensor(o_sb[:, lt, :], o_sb[:, lt, :], v, ALU.add).then_inc(o_part, 1)

                    multiply(0)
                    dve.tensor_tensor(o_sb[:, lt, :].rearrange("p (h d) -> p h d", h=H),
                                      own[:, D:2 * D].rearrange("p (h d) -> p h d", h=H),
                                      weights[:, NN, :].unsqueeze(2).to_broadcast([P, H, DH]), ALU.mult)\
                        .then_inc(o_part, 1)
                    for g in range(NG):
                        if g + 1 in DVE_V_GROUPS:
                            multiply(g + 1)
                        pair(g)
                        if g:
                            accumulate(g - 1)
                    accumulate(NG - 1)

                def attention(b):
                    for lt in range(TT):
                        keys(b, lt)
                        normalise(b, lt)
                        values(b, lt)

                def norms(b, second, tile_in, tile_out):
                    j0 = b * 2 * TT + second * TT

                    def norm_stats(t):
                        j = j0 + t
                        dve.wait_ge(ln_in, START + j + 1)
                        dve.bn_stats(stats[:, t % 2, :], tile_in(t)).then_inc(ln_part, 1)
                        dve.wait_ge(ln_part, START + j + 1)
                        dve.wait_ge(ln_out, START + j0 + max(t - 1, 0))
                        stand_alone(dve)
                        dve.bn_aggr(mean_var[:, t % 2, :], stats[:, t % 2, :]).then_inc(ln_stats, 1)

                    def norm_apply(t):
                        dve.wait_ge(ln_rstd, START + j0 + t + 1)
                        dve.tensor_scalar(tile_out(t), tile_in(t), mean_var[:, t % 2, 0:1], rstd[:, t % 2:t % 2 + 1],
                                          ALU.subtract, ALU.mult).then_inc(ln_out, 1)

                    norm_stats(0)
                    for t in range(TT):
                        if t + 1 < TT:
                            norm_stats(t + 1)
                        norm_apply(t)

                dve.wait_ge(consts2, START + CONSTS2)
                dve.tensor_copy(idx_f[:], idx_in[:]).then_inc(idx_step, 1)
                dve.wait_ge(idx_step, START + 1)
                dve.tensor_scalar(idx_t[:], idx_f[:], 0.0, float(NODES), ALU.is_lt, ALU.mult).then_inc(idx_step, 1)
                dve.wait_ge(idx_step, START + 2)
                dve.tensor_tensor(idx_f[:], idx_f[:], idx_t[:], ALU.add).then_inc(idx_step, 1)
                dve.wait_ge(idx_step, START + 3)
                dve.tensor_scalar(idx_f[:], idx_f[:], 0.0, float(NODES - 1), ALU.max, ALU.min).then_inc(idx_step, 1)
                dve.tensor_scalar(hide[:], mask_in[:].bitcast(U8), HIDE, None, ALU.mult).then_inc(hide_ready, 1)
                dve.wait_ge(hide_ready, START + 1)
                attention(0)

                def sequence(b, more):
                    norms(b, 0, lambda t: x2[:, t, :], lambda t: x2[:, t, :])
                    if more:
                        attention(b + 1)
                    norms(b, 1, lambda t: y3[:, t % 2, :], lambda t: y3[:, t % 2, :])

                with dve.Fori(0, B - 1) as b:
                    sequence(b, True)
                sequence(B - 1, False)

            @block.gpsimd
            def _(pool):
                def gather(b, lt, g):
                    n = b * (TT * NG) + lt * NG + g
                    back = n - SLOTS
                    if not isinstance(back, int) or back >= 0:
                        pool.wait_ge(o_part, START + back_parts(b, lt * NG + g - SLOTS))
                    stand_alone(pool)
                    for i in range(GN):
                        pool.indirect_dma_start(nb[:, slot(lt, g), i, :], None, kv_flat,
                                                bass.IndirectOffsetOnAxis(idx_rows[:, lt, g * GN + i:g * GN + i + 1], 0))\
                            .then_inc(gathered[slot(lt, g)], 16)

                def back_parts(b, i):
                    if i < 0:
                        b, i = b - 1, i + TT * NG
                    return b * (TT * (NG + 1)) + i // NG * (NG + 1) + i % NG + 2

                def rows(b):
                    if not (isinstance(b, int) and b == 0):
                        for s in gathered:
                            pool.wait_ge(s, b * (TT * NG // SLOTS * 16 * GN))
                        pool.wait_ge(idx_ready, START + b)
                        stand_alone(pool)
                        pool.tensor_scalar(idx_f[:], idx_f[:], float(FLAT), None, ALU.add).then_inc(idx_step, 1)
                    pool.wait_ge(idx_step, START + b + 4)
                    stand_alone(pool)
                    pool.tensor_copy(idx_rows[:], idx_f[:]).then_inc(idx_ready, 1)
                    pool.wait_ge(idx_ready, START + b + 1)

                def weight_values(b, lt):
                    n = b * TT + lt
                    pool.wait_ge(weights_ready, START + n + 1)
                    for g in POOL_V_GROUPS:
                        pool.wait_ge(gathered[slot(lt, g)], (16 * GN) * fills(b, lt, g))
                        vv = nb[:, slot(lt, g), :, D:2 * D].rearrange("p n (h d) -> p n h d", h=H)
                        w = weights[:, g * GN:(g + 1) * GN, :].unsqueeze(3).to_broadcast([P, GN, H, DH])
                        pool.tensor_tensor(vv, vv, w, ALU.mult).then_inc(v_mul_pool, 1)

                AHEAD = SLOTS - NG

                def first_gathers(b):
                    rows(b)
                    for i in range(SLOTS):
                        gather(b, i // NG, i % NG)

                def attention(b):
                    for lt in range(TT):
                        weight_values(b, lt)
                        for i in range((lt + 1) * NG + AHEAD, min((lt + 2) * NG + AHEAD, TT * NG)):
                            gather(b, i // NG, i % NG)

                def norms(b, second, tile, res, bias, wait_input):
                    j0 = b * 2 * TT + second * TT

                    def add(t):
                        j = j0 + t
                        wait_input(t)
                        pool.tensor_tensor(tile(t), tile(t), res(t), ALU.add).then_inc(ln_add, 1)
                        pool.wait_ge(ln_add, START + j + 1)
                        pool.tensor_tensor(tile(t), tile(t), bias, ALU.add).then_inc(ln_in, 1)

                    def rstd_of(t):
                        j = j0 + t
                        pool.wait_ge(ln_stats, START + j + 1)
                        pool.wait_ge(ln_rstd, START + j)
                        stand_alone(pool)
                        pool.tensor_scalar(var_eps[:], mean_var[:, t % 2, 1:2], EPS, None, ALU.add)\
                            .then_inc(ln_eps, 1)
                        pool.wait_ge(ln_eps, START + j + 2)
                        pool.tensor_tensor(rstd[:, t % 2:t % 2 + 1], var_eps[:], half[:], ALU.pow)\
                            .then_inc(ln_rstd, 1)

                    add(0)
                    for t in range(TT):
                        if t + 1 < TT:
                            add(t + 1)
                        rstd_of(t)

                pool.memset(half[:], -0.5).then_inc(ln_eps, 1)
                pool.wait_ge(ln_eps, START + 1)
                pool.wait_ge(consts2, START + CONSTS2)
                pool.wait_ge(idx_step, START + 4)
                first_gathers(0)
                attention(0)

                def sequence(b, more):
                    if more:
                        first_gathers(b + 1)

                    def tail_copied(lt):
                        pool.wait_ge(res_loaded, START + b * (16 * TT) + 16 * (lt + 1))
                        pool.wait_ge(work_free, item_copied(loop_item(b, I_TAIL + 2 * lt + 1)))

                    norms(b, 0, lambda t: x2[:, t, :], lambda t: x1_res[:], bo_sb[:], tail_copied)
                    if more:
                        attention(b + 1)
                    norms(b, 1, lambda t: y3[:, t % 2, :], lambda t: x2[:, t, :], b2_sb[:],
                          lambda t: pool.wait_ge(mlp_copied, START + b * TT + t + 1))

                with pool.Fori(0, B - 1) as b:
                    sequence(b, True)
                sequence(B - 1, False)


def rope_tables():
    freq = np.float32(1.0) / np.float32(10000.0) ** (np.arange(0, DH, 2, dtype=np.float32) / np.float32(DH))
    ang = (np.arange(T, dtype=np.float32)[:, None] * freq[None, :]).astype(np.float64)
    d = np.arange(P) % DH
    cos, sin = np.cos(ang)[:, d // 2].T, np.sin(ang)[:, d // 2].T * np.where(d % 2 == 0, -1.0, 1.0)[:, None]
    return np.stack([cos * (SCALE * Q_UP), sin * (SCALE * Q_UP), cos * K_UP, sin * K_UP]).astype(np.float32)


def node_scales():
    s, at, n = np.ones(FLAT, np.float32), T, T // 2
    for level in range(1, LEVELS + 1):
        s[at:at + n] = 0.5 ** level
        at, n = at + n, n // 2
    return np.ascontiguousarray(s.reshape(NT, P).T)


def kernel(x, ctx_1024, itok_Sx12_0_8189, mask_Sx12_bk0, L0_attn_W_qkv, L0_attn_b_qkv, L0_xattn_Wq, L0_xattn_Wk,
           L0_xattn_Wv, L0_xattn_Wo, L0_xattn_bo, L0_ffn_w1, L0_ffn_b1, L0_ffn_w2, L0_ffn_b2):
    import concourse.bacc as bacc
    from concourse.bass_utils import run_bass_kernel_spmd

    x, ctx = np.asarray(x), np.asarray(ctx_1024)
    b_qkv = np.asarray(L0_attn_b_qkv)
    arrays = {
        "x": x, "xT": x.transpose(0, 2, 1), "ctxT": ctx.transpose(0, 2, 1),
        "idx": np.asarray(itok_Sx12_0_8189), "mask": np.ascontiguousarray(mask_Sx12_bk0).view(np.int32),
        "wqkvT": np.asarray(L0_attn_W_qkv).T, "bqk": b_qkv[:2 * D].reshape(2 * KC, P).T, "bv": b_qkv[2 * D:],
        "wkT": np.asarray(L0_xattn_Wk).T, "wvT": np.asarray(L0_xattn_Wv).T, "wqT": np.asarray(L0_xattn_Wq).T,
        "woT": np.asarray(L0_xattn_Wo).T, "bo": np.asarray(L0_xattn_bo),
        "w1": np.asarray(L0_ffn_w1), "b1": np.asarray(L0_ffn_b1).reshape(WC, P).T,
        "w2": np.asarray(L0_ffn_w2), "b2": np.asarray(L0_ffn_b2),
        "rope": rope_tables(), "node_scale": node_scales(), "ident_in": np.eye(P, dtype=np.float32),
    }
    arrays = {f"in_{k}": np.ascontiguousarray(v) for k, v in arrays.items()}
    nc = bacc.Bacc("TRN2", target_bir_lowering=False, num_devices=1)
    args = [nc.dram_tensor(k, v.shape, mybir.dt.from_np(v.dtype), kind="ExternalInput").ap() for k, v in arrays.items()]
    out = nc.dram_tensor("out", (B, T, D), F32, kind="ExternalOutput").ap()
    decoder_layer(nc, *args, out)
    r = run_bass_kernel_spmd(nc, [arrays], core_ids=[0])
    return r.results[0]["out"]
```

```python
from contextlib import ExitStack

import numpy as np

import concourse.bass as bass
from concourse import mybir

F32 = mybir.dt.float32
F16 = mybir.dt.float16
I32 = mybir.dt.int32
U8 = mybir.dt.uint8
ALU = mybir.AluOpType
ACT = mybir.ActivationFunctionType
AX = mybir.AxisListType

P = 128
B = 8
T = 512
D = 512
H = 16
DH = D // H
TT = T // P
KC = D // P
NODES = 2 * T - 1
FLAT = 2 * T
NT = FLAT // P
LEVELS = 9
NN = 12
GN = 2
NG = NN // GN
SLOTS = 8
WIDTH = 2048
WC = WIDTH // P
EPS = 1e-5
SCALE = float(DH) ** -0.5
START = 1
HIDE = -1e30

Q_UP, K_UP = 64.0, 16.0
W_UP = 64.0
ROW_SCALE = 4096.0
ONES = DH
VW = DH + 1
SIDE = 64
M_ROW = 3 * DH
KS = M_ROW + 2

RING = 3
UNITS = TT * H
GROUP = UNITS // 4
M_LAG = GROUP + 2
E_LAG = GROUP + 8
PV_LAG = 2
PAIR = 2 * TT
O_COPY_LAG = E_LAG + PAIR - 1 + PV_LAG + 1
O_TURN_LAG = O_COPY_LAG + 1
PAIRS = UNITS // PAIR
STEPS = UNITS - PAIR + O_TURN_LAG + 1
MISC = 4 + PAIRS
V_SLOTS = (4, 10, E_LAG - 2, E_LAG - 1)
W1_PIECES = KC * WIDTH // D
W1_LOAD, W1_SPLIT, W1_STORE = (40, 58), (46, 66), (57, 74)
LOAD_SLOTS = (V_SLOTS[-1], V_SLOTS[-1] + 20)
TREE_SLOTS = tuple(E_LAG + 4 * t for t in range(2 * NT))
PROJECTIONS = (("qk", 0), ("qk", 1), ("kv", 0), ("qk", 2), ("kv", 1), ("qk", 3), ("kv", 2), ("qk", 4),
               ("qk", 5), ("kv", 3), ("qk", 6), ("kv", 4), ("qk", 7), ("kv", 5), ("kv", 6), ("kv", 7))


def ring_order():
    items = list(PROJECTIONS)
    for s in range(STEPS):
        items += [("v", V_SLOTS.index(s))] if s in V_SLOTS else []
        items += [("tree", TREE_SLOTS.index(s))] if s in TREE_SLOTS else []
        items += [("e", s - E_LAG)] if 0 <= s - E_LAG < UNITS else []
    return {item: number for number, item in enumerate(items)}


ITEM = ring_order()
N1 = len(ITEM)

RT = TT // 2
RW = RT * P
TURNS = 3 * RT
ORDER_O, ORDER_Q = (0, 2), (1, 3)
OUT_AT = 10
EXP_AT = (4, 12)
KEYS_AHEAD = 2
ROW_STEPS = 2
POOL_V_GROUPS = (3, 4, 5)
DVE_V_GROUPS = tuple(g for g in range(NG) if g not in POOL_V_GROUPS)


def misc_item(slot):
    if slot >= M_LAG and (slot - M_LAG) % GROUP == 0 and (slot - M_LAG) // GROUP < 4:
        return "max", (slot - M_LAG) // GROUP
    if slot >= O_TURN_LAG and (slot - O_TURN_LAG) % PAIR == 0 and (slot - O_TURN_LAG) // PAIR < PAIRS:
        return "out", (slot - O_TURN_LAG) // PAIR
    return None


MISC_SLOTS = [s for s in range(STEPS) if misc_item(s)]
MISC_OF_MAX = [MISC_SLOTS.index(M_LAG + g * GROUP) for g in range(4)]


def head_of(unit):
    return 4 * (unit % GROUP // TT) + unit // GROUP


def decoder_layer(nc, x, xT, ctxT, idx, mask, wqkvT, bqk, bv, wkT, wvT, wqT, woT, bo, w1, b1, w2, b2,
                  rope, node_scale, ident_in, out):
    outer = ExitStack()
    with outer:
        def alloc(stack):
            sems = []

            def sb(name, shape, dt=F32):
                return stack.enter_context(nc.sbuf_tensor(name, shape, dt))

            def sem(name):
                sems.append(stack.enter_context(nc.semaphore(name)))
                return sems[-1]
            return sb, sem, sems

        sb, sem, _ = alloc(outer)
        bank = [outer.enter_context(nc.psum_tensor(f"bank{i}", [P, 512], F32)) for i in range(8)]
        kv_flat = nc.dram_tensor("kv_flat", [B * FLAT, 2 * D], F32, kind="Internal").ap()
        w1_parts = [nc.dram_tensor(f"w1_{part}_dram", [W1_PIECES * P, D], F16, kind="Internal").ap()
                    for part in ("hi", "lo")]
        x1_dram = nc.dram_tensor("x1_dram", [B, T, D], F32, kind="Internal").ap()

        ident = sb("ident", [P, P])
        waits_passed = sem("waits_passed")

        def stand_alone(eng):
            eng.sem_inc(waits_passed, 1)

        def chunks(w):
            return w.rearrange("(c p) n -> p c n", p=P)

        def row(v):
            return v.rearrange("(a n) -> a n", a=1).to_broadcast((P, v.shape[0]))

        with ExitStack() as stack:
            sb, sem, sems = alloc(stack)
            w_hi = sb("w_hi", [P, 5, KC, D], F16)
            w_lo = sb("w_lo", [P, 5, KC, D], F16)
            rope_sb = sb("rope_sb", [P, 4, T])
            bqk_sb = sb("bqk_sb", [P, 2 * KC])
            bv_sb = sb("bv_sb", [P, D])
            scale_sb = sb("scale_sb", [P, NT])
            in_sb = sb("in_sb", [P, KC, T])
            in_hi = sb("in_hi", [P, 2, KC, T], F16)
            in_lo = sb("in_lo", [P, 2, KC, T], F16)
            xb = sb("xb", [P, TT, D])
            kvT = sb("kvT", [P, 2 * KC, FLAT])
            kv_nat = sb("kv_nat", [P, 2, D])
            raw = sb("raw", [P, 2, T])
            shuf = sb("shuf", [P, 2, T])
            rot = sb("rot", [P, 2, T])
            hi = sb("hi", [P, 2, KC, T], F16)
            lo = sb("lo", [P, 2, KC, T], F16)
            q_stack = sb("q_stack", [KS, H, T], F16)
            k_stack = sb("k_stack", [KS, H, T], F16)
            v_sb = sb("v_sb", [P, TT, H, VW])
            probsT = sb("probsT", [P, 3, T])
            neg_max = sb("neg_max", [P, 2, GROUP])
            max_hi = sb("max_hi", [GROUP, P], F16)
            max_lo = sb("max_lo", [GROUP, P], F16)
            oT = sb("oT", [P, T])
            inv_sum = sb("inv_sum", [P, TT, 2])
            attn = sb("attn", [P, TT, D])
            stats = sb("stats", [P, 2, 6])
            mean_var = sb("mean_var", [P, 2, 2])
            var_eps = sb("var_eps", [P, 1])
            rstd = sb("rstd", [P, 2])
            half = sb("half", [P, 1])
            w1_in = sb("w1_in", [P, D])
            w1_hi = sb("w1_hi", [P, D], F16)
            w1_lo = sb("w1_lo", [P, D], F16)

            consts_loaded, late_loaded = sem("consts_loaded"), sem("late_loaded")
            w_loaded = [sem(f"w_loaded_{w}") for w in ("q", "k", "xk", "xv", "v")]
            in_loaded, in_hi_done, in_split = sem("in_loaded"), sem("in_hi_done"), sem("in_split")
            w_hi_done, w_split, v_split = sem("w_hi_done"), sem("w_split"), sem("v_split")
            x_loaded = sem("x_loaded")
            w1_loaded, w1_hi_done, w1_lo_done, w1_stored = (sem("w1_loaded"), sem("w1_hi_done"), sem("w1_lo_done"),
                                                            sem("w1_stored"))
            work_ready, work_free = sem("work_ready"), sem("work_free")
            tree_level, xb_ready = sem("tree_level"), sem("xb_ready")
            rope_step, rot_done, hi_done, lo_done = sem("rope_step"), sem("rot_done"), sem("hi_done"), sem("lo_done")
            stacked = [sem(f"stacked{g}") for g in range(4)]
            kv_stored = [sem(f"kv_stored{i}") for i in range(2)]
            x1_stored = sem("x1_stored")
            rows_scored, max_done = sem("rows_scored"), sem("max_done")
            misc_ready, misc_free = sem("misc_ready"), sem("misc_free")
            max_hi_done, max_stacked = sem("max_hi_done"), sem("max_stacked")
            probs_used, pair_done, pair_copied = sem("probs_used"), sem("pair_done"), sem("pair_copied")
            inv_ready = sem("inv_ready")
            res_ready, ln_part, stats_ready = sem("res_ready"), sem("ln_part"), sem("stats_ready")
            rstd_part, rstd_ready, x1_ready = sem("rstd_part"), sem("rstd_ready"), sem("x1_ready")
            filled, pad_filled = sem("filled"), sem("pad_filled")
            ROWS, WORK, O, MB = bank[0:2], bank[2:5], bank[5:7], bank[7]
            CONSTS = 16 * 2
            LATE = 16 * 3
            FILLS = 4

            W_STAGE = [kvT[:, 2 * j:2 * j + 2, :].rearrange("p a (c n) -> p (a c) n", n=D)
                       for j in range(4)] + [attn[:]]

            def item_copied(b, item):
                return START + b * N1 + RING + item + 1

            block = stack.enter_context(nc.Block())

            @block.sync
            def _(sp):
                for s in sems:
                    sp.sem_inc(s, START)

                def load_in(b, which):
                    sp.wait_ge(in_split, START + b * 2 + which)
                    stand_alone(sp)
                    sp.dma_start(in_sb[:], (xT, ctxT)[which][bass.ds(b, 1)].rearrange("a (c p) t -> p (a c) t", p=P))\
                        .then_inc(in_loaded, 16)

                def load_x(b):
                    sp.dma_start(xb[:], x[bass.ds(b, 1)].rearrange("a (c p) d -> p (a c) d", p=P))\
                        .then_inc(x_loaded, 16)

                def load_w(j, w):
                    sp.dma_start(W_STAGE[j], w).then_inc(w_loaded[j], 16)

                load_in(0, 0)
                load_w(0, chunks(wqkvT)[:, :, 0:D])
                load_w(1, chunks(wqkvT)[:, :, D:2 * D])
                sp.dma_start(bqk_sb[:], bqk).then_inc(consts_loaded, 16)
                sp.dma_start(rope_sb[:], rope.rearrange("a p t -> p a t")).then_inc(consts_loaded, 16)
                load_w(2, chunks(wkT))
                load_in(0, 1)
                load_w(3, chunks(wvT))
                load_w(4, chunks(wqkvT)[:, :, 2 * D:])
                sp.dma_start(ident[:], ident_in).then_inc(late_loaded, 16)
                sp.dma_start(scale_sb[:], node_scale).then_inc(late_loaded, 16)
                sp.dma_start(bv_sb[:], row(bv)).then_inc(late_loaded, 16)
                load_x(0)

                def stack_heads(b, qk):
                    sp.wait_ge(lo_done, START + b * 2 * KC + (qk + 1) * KC)
                    sp.wait_ge(work_ready, START + b * N1)
                    parts = (hi, hi, lo) if qk == 0 else (hi, lo, hi)
                    dst = (q_stack, k_stack)[qk]
                    for g in range(4):
                        for i, part in enumerate(parts):
                            sp.dma_start(dst[i * DH:(i + 1) * DH, 4 * g:4 * g + 4, :],
                                         part[g * DH:(g + 1) * DH, qk, :, :]).then_inc(stacked[g], 16)

                def store_tree(b, t):
                    sp.wait_ge(work_free, item_copied(b, ITEM["tree", t]))
                    kv, n = t // NT, t % NT
                    sp.dma_start(kv_flat[bass.ds(b * FLAT + n * P, P), kv * D:(kv + 1) * D], kv_nat[:, t % 2, :])\
                        .then_inc(kv_stored[t % 2], 16)

                def stack_max(b, g):
                    sp.wait_ge(misc_free, START + b * MISC + MISC_OF_MAX[g] + 1)
                    for r, part in enumerate((max_hi, max_lo)):
                        sp.dma_start(q_stack[M_ROW + r:M_ROW + r + 1, 4 * g:4 * g + 4, :]
                                     .rearrange("a h (q t) -> a (h q) t", q=TT),
                                     part[:]).then_inc(max_stacked, 16)

                def store_x1(b):
                    for t in range(TT):
                        sp.wait_ge(x1_ready, START + b * TT + t + 1)
                        sp.dma_start(x1_dram[bass.ds(b, 1), t * P:(t + 1) * P, :].rearrange("a p d -> p (a d)"),
                                     attn[:, t, :]).then_inc(x1_stored, 16)

                def sequence(b, more):
                    stack_heads(b, 0)
                    stack_heads(b, 1)
                    for s in range(STEPS):
                        if more and s in LOAD_SLOTS:
                            load_in(b + 1, LOAD_SLOTS.index(s))
                        if s in TREE_SLOTS:
                            store_tree(b, TREE_SLOTS.index(s))
                        if s in W1_LOAD:
                            n = b * 2 + W1_LOAD.index(s)
                            sp.wait_ge(w1_lo_done, START + n)
                            stand_alone(sp)
                            sp.dma_start(w1_in[:], w1[bass.ds(n * P, P), :]).then_inc(w1_loaded, 16)
                        if s in W1_STORE:
                            n = b * 2 + W1_STORE.index(s)
                            sp.wait_ge(w1_lo_done, START + n + 1)
                            stand_alone(sp)
                            for dst, part in zip(w1_parts, (w1_hi, w1_lo)):
                                sp.dma_start(dst[bass.ds(n * P, P), :], part[:]).then_inc(w1_stored, 16)
                        what = misc_item(s)
                        if what and what[0] == "max":
                            stack_max(b, what[1])
                    store_x1(b)
                    if more:
                        load_x(b + 1)

                with sp.Fori(0, B - 1) as b:
                    sequence(b, True)
                sequence(B - 1, False)
                for s in kv_stored:
                    sp.wait_ge(s, START + 16 * B * 2 * NT // 2)
                sp.wait_ge(x1_stored, START + 16 * B * TT)
                sp.wait_ge(w1_stored, START + 2 * 16 * W1_PIECES)

            @block.tensor
            def _(pe):
                def take(b, item):
                    pe.wait_ge(work_free, START + b * N1 + max(item + 1, RING))
                    return WORK[item % RING]

                with pe.Fori(0, B) as b:
                    for kind, i in PROJECTIONS:
                        which, w = (0, i // KC) if kind == "qk" else (1, 2 + i // KC)
                        if i == 0:
                            pe.wait_ge(in_split, START + b * 2 + which + 1)
                        if i % KC == 0:
                            pe.wait_ge(w_split, START + w + 1)
                        o = take(b, ITEM[kind, i])
                        f = slice(i % KC * P, (i % KC + 1) * P)
                        for c in range(KC):
                            for k, (x_part, w_part) in enumerate(((in_hi, w_hi), (in_lo, w_hi), (in_hi, w_lo))):
                                mm = pe.matmul(o[:], w_part[:, w, c, f], x_part[:, which, c, :],
                                               start=c + k == 0, stop=c == KC - 1 and k == 2)
                        mm.then_inc(work_ready, 1)
                    pe.wait_ge(filled, START + FILLS)
                    pe.wait_ge(v_split, START + 3)
                    pe.wait_ge(late_loaded, START + LATE)
                    for s in range(STEPS):
                        if s in V_SLOTS:
                            t = V_SLOTS.index(s)
                            o = take(b, ITEM["v", t])
                            for c in range(KC):
                                for k, (x_part, w_part) in enumerate(((in_hi, w_hi), (in_hi, w_lo), (in_lo, w_hi))):
                                    mm = pe.matmul(o[:], x_part[:, 0, c, t * P:(t + 1) * P], w_part[:, 4, c, :],
                                                   start=c + k == 0, stop=c == KC - 1 and k == 2)
                            mm.then_inc(work_ready, 1)
                        if s in TREE_SLOTS:
                            t = TREE_SLOTS.index(s)
                            if t == 0:
                                pe.wait_ge(pad_filled, START + 1)
                                pe.wait_ge(tree_level, START + b * LEVELS + LEVELS)
                            kv, n = t // NT, t % NT
                            o = take(b, ITEM["tree", t])
                            for f in range(KC):
                                mm = pe.transpose(o[:, f * P:(f + 1) * P], kvT[:, kv * KC + f, n * P:(n + 1) * P],
                                                  ident[:])
                            mm.then_inc(work_ready, 1)
                        if s < UNITS:
                            h, qt = s // TT, s % TT
                            if s % GROUP == 0:
                                pe.wait_ge(stacked[s // GROUP], START + (b + 1) * (2 * 3 * 16))
                            pe.wait_ge(max_done, START + b * UNITS + max(s - 1, 0))
                            pe.matmul(ROWS[s % 2][:], q_stack[0:M_ROW, h, qt * P:(qt + 1) * P],
                                      k_stack[0:M_ROW, h, :], start=True, stop=True).then_inc(rows_scored, 1)
                        e = s - E_LAG
                        if 0 <= e < UNITS:
                            h, kt = e // TT, e % TT
                            if e % GROUP == 0:
                                pe.wait_ge(max_stacked, START + b * (4 * 32) + 32 * (e // GROUP + 1))
                            o = take(b, ITEM["e", e])
                            pe.matmul(o[:], k_stack[:, h, kt * P:(kt + 1) * P], q_stack[:, h, :],
                                      start=True, stop=True).then_inc(work_ready, 1)
                        e = s - E_LAG - PV_LAG
                        if 0 <= e < UNITS:
                            kt, side, pair = e % TT, e // TT % 2, e // PAIR
                            if e % PAIR == 0:
                                pe.wait_ge(pair_copied, START + b * PAIRS + max(pair - 1, 0))
                            pe.wait_ge(work_free, item_copied(b, ITEM["e", e]))
                            mm = pe.matmul(O[pair % 2][side * SIDE:side * SIDE + VW, :], v_sb[:, kt, head_of(e), :],
                                           probsT[:, e % 3, :], start=kt == 0, stop=kt == TT - 1)
                            mm.then_inc(pair_done if e % PAIR == PAIR - 1 else probs_used, 1)
                        what = misc_item(s)
                        if what:
                            pe.wait_ge(misc_free, START + b * MISC + MISC_SLOTS.index(s))
                            if what[0] == "max":
                                pe.wait_ge(max_done, START + b * UNITS + (what[1] + 1) * GROUP)
                                pe.transpose(MB[0:GROUP, 0:P], neg_max[:, what[1] % 2, :], ident[:])\
                                    .then_inc(misc_ready, 1)
                            else:
                                pe.wait_ge(pair_copied, START + b * PAIRS + what[1] + 1)
                                for t in range(TT):
                                    mm = pe.transpose(MB[:, t * P:(t + 1) * P], oT[:, t * P:(t + 1) * P], ident[:])
                                mm.then_inc(misc_ready, 1)

            @block.scalar
            def _(act):
                act.sem_inc(work_free, RING)
                def split(b, which):
                    act.wait_ge(in_loaded, START + (b * 2 + which) * 16 + 16)
                    act.activation(in_hi[:, which], in_sb[:], ACT.Copy).then_inc(in_hi_done, 1)

                split(0, 0)
                for j in range(4):
                    if j == 3:
                        split(0, 1)
                    act.wait_ge(w_loaded[j], START + 16)
                    act.activation(w_hi[:, j], W_STAGE[j], ACT.Copy, scale=W_UP).then_inc(w_hi_done, 1)
                act.wait_ge(consts_loaded, START + CONSTS)

                def sequence(b, more):
                    def item(i):
                        act.wait_ge(work_ready, START + b * N1 + i + 1)
                        return WORK[i % RING][:]

                    for kind, i in PROJECTIONS:
                        if kind == "qk":
                            act.wait_ge(rot_done, START + b * 2 * KC + max(i - 1, 0))
                            act.activation(raw[:, i % 2, :], item(ITEM["qk", i]), ACT.Identity, scale=1.0 / W_UP,
                                           bias=bqk_sb[:, i:i + 1]).then_inc(work_free, 1)
                        else:
                            act.activation(kvT[:, i, 0:T], item(ITEM["kv", i]), ACT.Copy, scale=1.0 / W_UP)\
                                .then_inc(work_free, 1)
                    act.wait_ge(late_loaded, START + LATE)
                    for s in range(STEPS):
                        if s in V_SLOTS:
                            t = V_SLOTS.index(s)
                            act.activation(v_sb[:, t, :, 0:DH], item(ITEM["v", t]).rearrange("p (h d) -> p h d", h=H),
                                           ACT.Copy, scale=1.0 / W_UP).then_inc(work_free, 1)
                        if s in TREE_SLOTS:
                            t = TREE_SLOTS.index(s)
                            src = item(ITEM["tree", t])
                            act.wait_ge(kv_stored[t % 2], START + b * (16 * 2 * NT // 2) + 16 * (t // 2))
                            if t < NT:
                                act.activation(kv_nat[:, t % 2, :], src, ACT.Copy, scale=scale_sb[:, t:t + 1])\
                                    .then_inc(work_free, 1)
                            else:
                                act.activation(kv_nat[:, t % 2, :], src, ACT.Copy).then_inc(work_free, 1)
                        e = s - E_LAG
                        if 0 <= e < UNITS:
                            src = item(ITEM["e", e])
                            act.activation(probsT[:, e % 3, :], src, ACT.Exp, scale=1.0 / (Q_UP * K_UP))\
                                .then_inc(work_free, 1)
                        p = s - O_COPY_LAG
                        if p >= 0 and p % PAIR == 0 and p // PAIR < PAIRS:
                            p //= PAIR
                            act.wait_ge(pair_done, START + b * PAIRS + p + 1)
                            before = MISC_SLOTS.index(O_TURN_LAG + PAIR * (p - 1)) + 1 if p else 0
                            act.wait_ge(misc_ready, START + b * MISC + before)
                            act.activation(oT[:], O[p % 2][:], ACT.Copy).then_inc(pair_copied, 1)
                        if s in W1_SPLIT:
                            n = b * 2 + W1_SPLIT.index(s)
                            act.wait_ge(w1_loaded, START + n * 16 + 16)
                            act.wait_ge(w1_stored, START + n * 32)
                            act.activation(w1_in[:], w1_in[:], ACT.Copy, scale=W_UP).then_inc(w1_hi_done, 1)
                            act.wait_ge(w1_hi_done, START + 2 * n + 1)
                            act.activation(w1_hi[:], w1_in[:], ACT.Copy).then_inc(w1_hi_done, 1)
                        if more and s - 8 in LOAD_SLOTS:
                            split(b + 1, LOAD_SLOTS.index(s - 8))

                with act.Fori(0, B - 1) as b:
                    sequence(b, True)
                sequence(B - 1, False)

            @block.vector
            def _(dve):
                for o in O:
                    dve.memset(o[:], 0.0).then_inc(filled, 1)
                dve.memset(v_sb[:, :, :, ONES:ONES + 1], 1.0).then_inc(filled, 1)
                dve.memset(k_stack[M_ROW:KS, :, :], ROW_SCALE).then_inc(filled, 1)
                for j in range(4):
                    dve.wait_ge(w_hi_done, START + j + 1)
                    dve.scalar_tensor_tensor(out=w_lo[:, j], in0=W_STAGE[j], scalar=W_UP, in1=w_hi[:, j],
                                             op0=ALU.mult, op1=ALU.subtract).then_inc(w_split, 1)
                dve.wait_ge(consts_loaded, START + CONSTS)
                swap = [i ^ 1 for i in range(32)]
                with dve.Fori(0, B) as b:
                    for i in range(2 * KC):
                        qk, c, n = i // KC, i % KC, b * 2 * KC + i
                        cos, sin = rope_sb[:, 2 * qk, :], rope_sb[:, 2 * qk + 1, :]
                        sh, ro, r = shuf[:, i % 2, :], rot[:, i % 2, :], raw[:, i % 2, :]
                        dve.wait_ge(work_free, item_copied(b, ITEM["qk", i]))
                        dve.wait_ge(rot_done, START + b * 2 * KC + max(i - 1, 0))
                        dve.wait_ge(lo_done, START + b * 2 * KC + max(i - 1, 0))
                        stand_alone(dve)
                        dve.stream_shuffle(sh, r, swap).then_inc(rope_step, 1)
                        dve.tensor_tensor(ro, r, cos, ALU.mult).then_inc(rope_step, 1)
                        dve.wait_ge(rope_step, START + b * 6 * KC + 3 * i + 1)
                        dve.tensor_tensor(sh, sh, sin, ALU.mult).then_inc(rope_step, 1)
                        dve.wait_ge(rope_step, START + b * 6 * KC + 3 * i + 3)
                        dve.tensor_tensor(ro, ro, sh, ALU.add).then_inc(rot_done, 1)
                        dve.wait_ge(rot_done, START + n + 1)
                        if i == 0:
                            for s in stacked:
                                dve.wait_ge(s, START + b * (2 * 3 * 16))
                        dve.tensor_copy(hi[:, qk, c, :], ro).then_inc(hi_done, 1)
                    for s in range(STEPS):
                        if s < UNITS:
                            g, at = s // GROUP, s % GROUP
                            dve.wait_ge(rows_scored, START + b * UNITS + s + 1)
                            dve.tensor_reduce(neg_max[:, g % 2, at:at + 1], ROWS[s % 2][:], AX.X, ALU.max,
                                              negate=True).then_inc(max_done, 1)
                        what = misc_item(s)
                        if what and what[0] == "max":
                            n = b * 4 + what[1]
                            dve.wait_ge(misc_ready, START + b * MISC + MISC_SLOTS.index(s) + 1)
                            dve.wait_ge(max_stacked, START + n * 32)
                            dve.tensor_scalar(max_hi[:], MB[0:GROUP, 0:P], 1.0 / ROW_SCALE, None, ALU.mult)\
                                .then_inc(max_hi_done, 1)
                            dve.wait_ge(max_hi_done, START + n + 1)
                            dve.scalar_tensor_tensor(out=max_lo[:], in0=MB[0:GROUP, 0:P], scalar=1.0 / ROW_SCALE,
                                                     in1=max_hi[:], op0=ALU.mult, op1=ALU.subtract)\
                                .then_inc(misc_free, 1)
                        if what and what[0] == "out":
                            p = what[1]
                            n = b * PAIRS + p
                            dve.wait_ge(misc_ready, START + b * MISC + MISC_SLOTS.index(s) + 1)
                            pair = MB[:].rearrange("p (t s w) -> p t s w", t=TT, s=2)
                            dve.wait_ge(misc_free, START + b * MISC + MISC_SLOTS.index(s))
                            dve.reciprocal(inv_sum[:].unsqueeze(3), pair[:, :, :, ONES:ONES + 1])\
                                .then_inc(inv_ready, 1)
                            dve.wait_ge(inv_ready, START + n + 1)
                            dve.wait_ge(x1_stored, START + b * (16 * TT))
                            h = head_of(p * PAIR)
                            cols = attn[:].rearrange("p t (h d) -> p t h d", h=H)[:, :, h:h + 5:4, :]
                            dve.tensor_tensor(cols, pair[:, :, :, 0:DH],
                                              inv_sum[:].unsqueeze(3).to_broadcast([P, TT, 2, DH]),
                                              ALU.mult).then_inc(misc_free, 1)

                    def norm_stats(t):
                        n = b * TT + t
                        dve.wait_ge(res_ready, START + n + 1)
                        dve.bn_stats(stats[:, t % 2, :], attn[:, t, :]).then_inc(ln_part, 1)
                        dve.wait_ge(ln_part, START + n + 1)
                        dve.wait_ge(x1_ready, START + b * TT + max(t - 1, 0))
                        stand_alone(dve)
                        dve.bn_aggr(mean_var[:, t % 2, :], stats[:, t % 2, :]).then_inc(stats_ready, 1)

                    def norm_apply(t):
                        dve.wait_ge(rstd_ready, START + b * TT + t + 1)
                        dve.tensor_scalar(attn[:, t, :], attn[:, t, :], mean_var[:, t % 2, 0:1],
                                          rstd[:, t % 2:t % 2 + 1], ALU.subtract, ALU.mult).then_inc(x1_ready, 1)

                    norm_stats(0)
                    for t in range(TT):
                        if t + 1 < TT:
                            norm_stats(t + 1)
                        norm_apply(t)

            @block.gpsimd
            def _(pool):
                pool.memset(half[:], -0.5).then_inc(rstd_part, 1)

                def split(b, which):
                    n = b * 2 + which
                    pool.wait_ge(in_hi_done, START + n + 1)
                    pool.tensor_tensor(in_lo[:, which], in_sb[:], in_hi[:, which], ALU.subtract).then_inc(in_split, 1)

                split(0, 0)
                split(0, 1)
                pool.wait_ge(w_loaded[4], START + 16)
                stand_alone(pool)
                pool.tensor_scalar(W_STAGE[4], W_STAGE[4], W_UP, None, ALU.mult).then_inc(v_split, 1)
                pool.wait_ge(v_split, START + 1)
                stand_alone(pool)
                pool.tensor_copy(w_hi[:, 4], W_STAGE[4]).then_inc(v_split, 1)
                pool.wait_ge(v_split, START + 2)
                pool.tensor_tensor(w_lo[:, 4], W_STAGE[4], w_hi[:, 4], ALU.subtract).then_inc(v_split, 1)
                pool.wait_ge(w_split, START + 4)
                pool.memset(kvT[:, :, FLAT - 1:FLAT], 0.0).then_inc(pad_filled, 1)
                pool.wait_ge(late_loaded, START + LATE)
                pool.wait_ge(rstd_part, START + 1)

                def sequence(b, more):
                    for i in range(2 * KC):
                        n, ro = b * 2 * KC + i, rot[:, i % 2, :]
                        pool.wait_ge(hi_done, START + n + 1)
                        pool.tensor_tensor(lo[:, i // KC, i % KC, :], ro, hi[:, i // KC, i % KC, :], ALU.subtract)\
                            .then_inc(lo_done, 1)
                    pool.wait_ge(work_free, item_copied(b, ITEM["kv", 2 * KC - 1]))
                    src, n = 0, T
                    for level in range(LEVELS):
                        if level:
                            pool.wait_ge(tree_level, START + b * LEVELS + level)
                        pool.tensor_tensor(kvT[:, :, src + n:src + n + n // 2], kvT[:, :, src:src + n:2],
                                           kvT[:, :, src + 1:src + n:2], ALU.add).then_inc(tree_level, 1)
                        src, n = src + n, n // 2
                    pool.wait_ge(x_loaded, START + b * 16 + 16)
                    for t in range(TT):
                        pool.tensor_tensor(xb[:, t, :], xb[:, t, :], bv_sb[:], ALU.add).then_inc(xb_ready, 1)

                    def add_residual(t):
                        pool.tensor_tensor(attn[:, t, :], attn[:, t, :], xb[:, t, :], ALU.add).then_inc(res_ready, 1)

                    def rstd_of(t):
                        n = b * TT + t
                        pool.wait_ge(stats_ready, START + n + 1)
                        pool.wait_ge(rstd_ready, START + n)
                        stand_alone(pool)
                        pool.tensor_scalar(var_eps[:], mean_var[:, t % 2, 1:2], EPS, None, ALU.add)\
                            .then_inc(rstd_part, 1)
                        pool.wait_ge(rstd_part, START + n + 2)
                        pool.tensor_tensor(rstd[:, t % 2:t % 2 + 1], var_eps[:], half[:], ALU.pow)\
                            .then_inc(rstd_ready, 1)

                    if more:
                        split(b + 1, 0)
                        split(b + 1, 1)
                    for j in range(2):
                        n = b * 2 + j
                        pool.wait_ge(w1_hi_done, START + 2 * n + 2)
                        pool.tensor_tensor(w1_lo[:], w1_in[:], w1_hi[:], ALU.subtract).then_inc(w1_lo_done, 1)
                    pool.wait_ge(xb_ready, START + b * TT + TT)
                    pool.wait_ge(misc_free, START + b * MISC + MISC)
                    add_residual(0)
                    for t in range(TT):
                        if t + 1 < TT:
                            add_residual(t + 1)
                        rstd_of(t)

                with pool.Fori(0, B - 1) as b:
                    sequence(b, True)
                sequence(B - 1, False)

        with ExitStack() as stack:
            sb, sem, sems = alloc(stack)
            w1_sb = [sb(f"w1_{part}_sb", [P, KC, WIDTH], F16) for part in ("hi", "lo")]
            w2_sb = sb("w2_sb", [P, WC, D])
            wq_sb = sb("wq_sb", [P, KC, D])
            wo_sb = sb("wo_sb", [P, KC, D])
            b1_sb = sb("b1_sb", [P, WC])
            bo_sb = sb("bo_sb", [P, D])
            b2_sb = sb("b2_sb", [P, D])
            idx_in = sb("idx_in", [P, TT, NN], I32)
            idx_f = sb("idx_f", [P, TT, NN])
            idx_t = sb("idx_t", [P, TT, NN])
            idx_rows = sb("idx_rows", [P, TT, NN], I32)
            mask_in = sb("mask_in", [P, TT, NN // 4], I32)
            hide = sb("hide", [P, TT, NN])
            nb = sb("nb", [P, SLOTS, GN, 2 * D])
            own = sb("own", [P, 2 * D])
            q_sb = sb("q_sb", [P, TT, D])
            logits = sb("logits", [P, 2, NN + 1, H])
            top = sb("top", [P, H])
            weights = sb("weights", [P, NN + 1, H])
            total = sb("total", [P, H])
            o_sb = sb("o_sb", [P, 2, D])
            x1_in = sb("x1_in", [P, 2, D])
            x1_res = sb("x1_res", [P, D])
            actT = sb("actT", [P, 2, KC, P])
            x2 = sb("x2", [P, TT, D])
            x2b = sb("x2b", [P, TT, D])
            x2T_hi = sb("x2T_hi", [P, KC, T], F16)
            x2T_lo = sb("x2T_lo", [P, KC, T], F16)
            hid = sb("hid", [P, 2, RW])
            stats = sb("stats2", [P, 2, 6])
            mean_var = sb("mean_var2", [P, 2, 2])
            var_eps = sb("var_eps2", [P, 1])
            rstd = sb("rstd2", [P, 2])
            half = sb("half2", [P, 1])

            consts2, idx_loaded, w_loaded = sem("consts2"), sem("idx_loaded"), sem("w_loaded")
            CONSTS2 = 16 * 4
            WEIGHTS = 16 * 3
            idx_step, idx_ready, hide_ready = sem("idx_step"), sem("idx_ready"), sem("hide_ready")
            wo_loaded = sem("wo_loaded")
            gathered = [sem(f"gathered{i}") for i in range(SLOTS)]
            own_loaded, res_loaded, res_ready = sem("own_loaded"), sem("res_loaded"), sem("res_ready2")
            k_mul, k_sum = sem("k_mul"), sem("k_sum")
            max_step, shifted, exp_done = sem("max_step"), sem("shifted"), sem("exp_done")
            norm_step, weights_ready = sem("norm_step"), sem("weights_ready")
            v_mul_dve, v_mul_pool, v_pair, o_part = sem("v_mul_dve"), sem("v_mul_pool"), sem("v_pair"), sem("o_part")
            x1_loaded = [sem("x1_loaded0"), sem("x1_loaded1")]
            turn_ready, turn_copied = sem("turn_ready"), sem("turn_copied")
            proj_ready, q_copied, out_added = sem("proj_ready"), sem("q_copied"), sem("out_added")
            ln_part, ln_stats = sem("ln_part2"), sem("ln_stats")
            ln_eps, ln_rstd, ln_out = sem("ln_eps"), sem("ln_rstd"), sem("ln_out")
            h_psum, h_ready = sem("h_psum"), sem("h_ready")
            x2b_ready, mlp_ready, y_added = sem("x2b_ready"), sem("mlp_ready"), sem("y_added")
            x2_split = sem("x2_split")
            out_stored = [sem("out_stored0"), sem("out_stored1")]
            TURN, PROJ, HB, ACC = bank[0], bank[1], bank[2:4], bank[4:8]
            X2_TURN = (TURN, HB[0])

            def round_of(b, lt):
                return b * 2 + lt // RT

            def is_first(b, lt):
                return isinstance(b, int) and b == 0 and lt < RT

            def is_last(b, lt):
                return isinstance(b, int) and b == B - 1 and lt >= RT

            def order_o(b, lt):
                return lt % RT if is_last(b, lt) else ORDER_O[lt % RT]

            def order_q(b, lt):
                return lt if is_first(b, lt) else ORDER_Q[lt % RT]

            def before(order, place):
                return sum(o < place for o in order)

            def turn_o(b, lt):
                return RT + round_of(b, lt) * TURNS + order_o(b, lt)

            def turn_q(b, lt):
                return lt if is_first(b, lt) else RT + (round_of(b, lt) - 1) * TURNS + ORDER_Q[lt % RT]

            def turn_x2(b, lt):
                return RT + round_of(b, lt) * TURNS + (RT if is_last(b, lt) else 2 * RT) + lt % RT

            def proj_o(b, lt):
                return RT + round_of(b, lt) * 2 * RT + order_o(b, lt)

            def proj_q(b, lt):
                return lt if is_first(b, lt) else RT + (round_of(b, lt) - 1) * 2 * RT + ORDER_Q[lt % RT]

            def norm_x2(b, lt):
                if is_first(b, lt):
                    return lt
                return RT + (round_of(b, lt) - 1) * 2 * RT + (0 if lt % RT == 0 else 2 * RT - 1)

            def norm_y(b, lt):
                return RT + round_of(b, lt) * 2 * RT + (0 if is_last(b, lt) else 1) + lt % RT

            def y_slot(b, lt):
                return (lt if is_last(b, lt) else lt + 1) % 2

            def next_round(b, half):
                return (b, 1) if half == 0 else (b + 1, 0)

            def last_round(b, half):
                return (b, 0) if half == 1 else (b - 1, 1)

            def tiles(half):
                return range(half * RT, half * RT + RT)

            def actT_slot(order):
                return order % 2

            def slot(lt, g):
                return (lt * NG + g) % SLOTS

            def fills(b, lt, g):
                return b * (TT * NG // SLOTS) + (lt * NG + g) // SLOTS + 1

            block = stack.enter_context(nc.Block())

            @block.sync
            def _(sp):
                for s in sems:
                    if s not in gathered:
                        sp.sem_inc(s, START)

                def load_x1(b, lt):
                    if lt > 1:
                        sp.wait_ge(turn_ready, START + turn_q(b, lt - 2) + 1)
                        stand_alone(sp)
                    elif not (isinstance(b, int) and b == 0):
                        last = turn_q(0 if isinstance(b, int) and b == 1 else b - 1, lt + 2)
                        sp.wait_ge(turn_ready, START + last + 1)
                        stand_alone(sp)
                    sp.dma_start(x1_in[:, lt % 2, :],
                                 x1_dram[bass.ds(b, 1), lt * P:(lt + 1) * P, :].rearrange("a p d -> p (a d)"))\
                        .then_inc(x1_loaded[lt % 2], 16)

                def load_own(b, lt):
                    if lt or not isinstance(b, int):
                        sp.wait_ge(o_part, START + b * (TT * (NG + 1)) + (lt - 1) * (NG + 1) + 1)
                        stand_alone(sp)
                    elif b:
                        sp.wait_ge(o_part, START + b * (TT * (NG + 1)) - NG)
                    sp.dma_start(own[:], kv_flat[bass.ds(b * FLAT + lt * P, P), :]).then_inc(own_loaded, 16)

                def load_res(b, lt):
                    sp.wait_ge(out_added, START + b * TT + lt)
                    stand_alone(sp)
                    sp.dma_start(x1_res[:],
                                 x1_dram[bass.ds(b, 1), lt * P:(lt + 1) * P, :].rearrange("a p d -> p (a d)"))\
                        .then_inc(res_loaded, 16)

                def store(b, half):
                    for lt in tiles(half):
                        sp.wait_ge(ln_out, START + norm_y(b, lt) + 1)
                        stand_alone(sp)
                        sp.dma_start(out[bass.ds(b, 1), lt * P:(lt + 1) * P, :].rearrange("a p d -> p (a d)"),
                                     x2b[:, lt, :]).then_inc(out_stored[half], 16)

                def round_moves(b, half, ahead):
                    lt = half * RT
                    load_own(b, lt + 1)
                    load_res(b, lt + 1)
                    nb_, nh = next_round(b, half)
                    if ahead > 0:
                        load_own(nb_, nh * RT)
                        load_res(nb_, nh * RT)
                    if not is_first(b, lt):
                        store(*last_round(b, half))
                    if ahead > 1:
                        fb, fh = next_round(nb_, nh)
                        load_x1(fb, fh * RT)
                        load_x1(fb, fh * RT + 1)

                sp.dma_start(idx_in[:], idx.rearrange("(c p) n -> p c n", p=P)).then_inc(idx_loaded, 16)
                sp.dma_start(mask_in[:], mask.rearrange("(c p) n -> p c n", p=P)).then_inc(idx_loaded, 16)
                load_x1(0, 0)
                load_x1(0, 1)
                sp.dma_start(wq_sb[:], chunks(wqT)).then_inc(consts2, 16)
                sp.dma_start(bo_sb[:], row(bo)).then_inc(consts2, 16)
                sp.dma_start(b1_sb[:], b1).then_inc(consts2, 16)
                sp.dma_start(b2_sb[:], row(b2)).then_inc(consts2, 16)
                load_own(0, 0)
                load_res(0, 0)
                load_x1(0, 2)
                load_x1(0, 3)
                sp.dma_start(wo_sb[:], chunks(woT)).then_inc(wo_loaded, 16)
                sp.wait_ge(k_sum, START + NG + 1)
                for dst, part in zip(w1_sb, w1_parts):
                    sp.dma_start(dst[:].rearrange("p c (n m) -> p c n m", m=D),
                                 part.rearrange("(c n p) m -> p c n m", p=P, c=KC)).then_inc(w_loaded, 16)
                sp.dma_start(w2_sb[:], chunks(w2)).then_inc(w_loaded, 16)
                round_moves(0, 0, 2)
                with sp.Fori(0, B - 2) as b:
                    round_moves(b, 1, 2)
                    round_moves(b + 1, 0, 2)
                round_moves(B - 2, 1, 2)
                round_moves(B - 1, 0, 1)
                round_moves(B - 1, 1, 0)
                store(B - 1, 1)
                for s in out_stored:
                    sp.wait_ge(s, START + 16 * B * RT)

            @block.tensor
            def _(pe):
                def turn(bank_, tile):
                    for f in range(KC):
                        mm = pe.transpose(bank_[:, f * P:(f + 1) * P], tile[:, f * P:(f + 1) * P], ident[:])
                    mm.then_inc(turn_ready, 1)

                def turn_out(b, lt):
                    pe.wait_ge(turn_copied, START + turn_o(b, lt))
                    pe.wait_ge(o_part, START + b * (TT * (NG + 1)) + (lt + 1) * (NG + 1))
                    turn(TURN, o_sb[:, lt % 2, :])

                def turn_query(b, lt):
                    pe.wait_ge(turn_copied, START + turn_q(b, lt))
                    pe.wait_ge(x1_loaded[lt % 2], START + b * (16 * TT // 2) + 16 * (lt // 2 + 1))
                    turn(TURN, x1_in[:, lt % 2, :])

                def project_out(b, lt):
                    pe.wait_ge(turn_copied, START + turn_o(b, lt) + 1)
                    q_before = 0 if is_last(b, lt) else before(ORDER_Q, ORDER_O[lt % RT])
                    pe.wait_ge(out_added, START + b * TT + lt)
                    pe.wait_ge(q_copied, START + (round_of(b, lt) + 1) * RT + q_before)
                    for c in range(KC):
                        mm = pe.matmul(PROJ[:], actT[:, actT_slot(order_o(b, lt)), c, :], wo_sb[:, c, :],
                                       start=c == 0, stop=c == KC - 1)
                    mm.then_inc(proj_ready, 1)

                def project_query(b, lt):
                    pe.wait_ge(turn_copied, START + turn_q(b, lt) + 1)
                    pe.wait_ge(q_copied, START + b * TT + lt)
                    if not is_first(b, lt):
                        pe.wait_ge(out_added, START + (round_of(b, lt) - 1) * RT + before(ORDER_O, ORDER_Q[lt % RT]))
                    for c in range(KC):
                        mm = pe.matmul(PROJ[:], actT[:, actT_slot(order_q(b, lt)), c, :], wq_sb[:, c, :],
                                       start=c == 0, stop=c == KC - 1)
                    mm.then_inc(proj_ready, 1)

                def round_end(b, half, more):
                    first, second = tiles(half)
                    qb, qh = next_round(b, half)
                    if more:
                        project_query(qb, qh * RT)
                    turn_out(b, second)
                    if more:
                        turn_query(qb, qh * RT + 1)
                    project_out(b, second)
                    for lt in (first, second):
                        if lt == first:
                            pe.wait_ge(turn_copied, START + turn_x2(b, lt))
                        elif more:
                            project_query(qb, qh * RT + 1)
                        pe.wait_ge(ln_out, START + norm_x2(b, lt) + 1)
                        turn(X2_TURN[lt % RT], x2[:, lt, :])
                    pe.wait_ge(x2_split, START + b * TT + second + 1)

                def hidden(b, half, c):
                    pe.wait_ge(h_ready, START + (b * 2 + half) * WC + max(c - 1, 0))
                    for k in range(KC):
                        for i, (w, x_part) in enumerate(((w1_sb[0], x2T_hi), (w1_sb[0], x2T_lo), (w1_sb[1], x2T_hi))):
                            mm = pe.matmul(HB[c % 2][:, 0:RW], w[:, k, c * P:(c + 1) * P],
                                           x_part[:, k, half * RW:(half + 1) * RW],
                                           start=k + i == 0, stop=k == KC - 1 and i == 2)
                    mm.then_inc(h_psum, 1)

                def mlp_out(b, half, c):
                    pe.wait_ge(h_ready, START + (b * 2 + half) * WC + c + 1)
                    for lt in tiles(half):
                        i = lt % RT
                        mm = pe.matmul(ACC[lt][:], hid[:, c % 2, i * P:(i + 1) * P], w2_sb[:, c, :],
                                       start=c == 0, stop=c == WC - 1)
                    if c == WC - 1:
                        mm.then_inc(mlp_ready, 1)

                def mlp(b, half, attend, more):
                    ab, ah = next_round(b, half)
                    hidden(b, half, 0)
                    for c in range(1, WC):
                        hidden(b, half, c)
                        if attend and c == OUT_AT:
                            turn_out(ab, ah * RT)
                        mlp_out(b, half, c - 1)
                        if attend and c == OUT_AT:
                            project_out(ab, ah * RT)
                    if more:
                        qb, qh = next_round(ab, ah)
                        turn_query(qb, qh * RT)
                    mlp_out(b, half, WC - 1)
                    if attend:
                        round_end(ab, ah, more)

                pe.wait_ge(consts2, START + CONSTS2)
                for lt in range(RT):
                    turn_query(0, lt)
                    project_query(0, lt)
                pe.wait_ge(wo_loaded, START + 16)
                turn_out(0, 0)
                project_out(0, 0)
                turn_query(0, RT)
                round_end(0, 0, True)
                pe.wait_ge(w_loaded, START + WEIGHTS)
                with pe.Fori(0, B - 1) as b:
                    mlp(b, 0, True, True)
                    mlp(b, 1, True, True)
                mlp(B - 1, 0, True, False)
                mlp(B - 1, 1, False, False)

            @block.scalar
            def _(act):
                act.wait_ge(consts2, START + CONSTS2)

                def turned(k, order):
                    act.wait_ge(turn_ready, START + k + 1)
                    act.activation(actT[:, actT_slot(order)].rearrange("p c t -> p (c t)"), TURN[:], ACT.Copy)\
                        .then_inc(turn_copied, 1)

                def turned_out(b, lt):
                    turned(turn_o(b, lt), order_o(b, lt))

                def turned_query(b, lt):
                    turned(turn_q(b, lt), order_q(b, lt))

                def query(b, lt):
                    act.wait_ge(proj_ready, START + proj_q(b, lt) + 1)
                    if not (isinstance(b, int) and b == 0):
                        act.wait_ge(k_sum, START + (b - 1) * (TT * (NG + 1)) + (lt + 1) * (NG + 1))
                    act.activation(q_sb[:, lt, :], PROJ[:], ACT.Copy, scale=SCALE).then_inc(q_copied, 1)

                def exponentials(b, lt):
                    act.wait_ge(shifted, START + b * TT + lt + 1)
                    act.activation(weights[:].rearrange("p n h -> p (n h)"),
                                   logits[:, lt % 2].rearrange("p n h -> p (n h)"), ACT.Exp).then_inc(exp_done, 1)

                def round_end(b, half, more):
                    first, second = tiles(half)
                    qb, qh = next_round(b, half)
                    if more:
                        query(qb, qh * RT)
                    turned_out(b, second)
                    if more:
                        turned_query(qb, qh * RT + 1)
                    for lt in (first, second):
                        if lt == second and more:
                            query(qb, qh * RT + 1)
                        act.wait_ge(turn_ready, START + turn_x2(b, lt) + 1)
                        act.activation(x2T_hi[:, :, lt * P:(lt + 1) * P],
                                       X2_TURN[lt % RT][:].rearrange("p (c t) -> p c t", c=KC), ACT.Copy)\
                            .then_inc(turn_copied, 1)

                def mlp(b, half, attend, more):
                    ab, ah = next_round(b, half)
                    for c in range(WC):
                        act.wait_ge(h_psum, START + (b * 2 + half) * WC + c + 1)
                        act.activation(hid[:, c % 2, :], HB[c % 2][:, 0:RW], ACT.Relu, scale=1.0 / W_UP,
                                       bias=b1_sb[:, c:c + 1])\
                            .then_inc(h_ready, 1)
                        if attend and c == OUT_AT:
                            turned_out(ab, ah * RT)
                        if attend and c in EXP_AT:
                            exponentials(ab, ah * RT + EXP_AT.index(c))
                    if more:
                        qb, qh = next_round(ab, ah)
                        turned_query(qb, qh * RT)
                    if attend:
                        round_end(ab, ah, more)

                for lt in range(RT):
                    turned_query(0, lt)
                    query(0, lt)
                exponentials(0, 0)
                turned_out(0, 0)
                turned_query(0, RT)
                exponentials(0, 1)
                round_end(0, 0, True)
                with act.Fori(0, B - 1) as b:
                    mlp(b, 0, True, True)
                    mlp(b, 1, True, True)
                mlp(B - 1, 0, True, False)
                mlp(B - 1, 1, False, False)

            @block.vector
            def _(dve):
                def key_sums(b, lt, groups):
                    n = b * TT + lt
                    q = q_sb[:, lt, :]
                    dve.wait_ge(q_copied, START + n + 1)

                    def multiply(g):
                        if g < NG:
                            dve.wait_ge(gathered[slot(lt, g)], (16 * GN) * fills(b, lt, g))
                            kk = nb[:, slot(lt, g), :, 0:D]
                            dve.tensor_tensor(kk, kk, q.unsqueeze(1).to_broadcast([P, GN, D]), ALU.mult)\
                                .then_inc(k_mul, 1)
                        else:
                            dve.wait_ge(own_loaded, START + n * 16 + 16)
                            dve.tensor_tensor(own[:, 0:D], own[:, 0:D], q, ALU.mult).then_inc(k_mul, 1)

                    def reduce(g):
                        dve.wait_ge(k_mul, START + n * (NG + 1) + g + 1)
                        if g < NG:
                            dve.tensor_reduce(logits[:, lt % 2, g * GN:(g + 1) * GN, :],
                                              nb[:, slot(lt, g), :, 0:D].rearrange("p n (h d) -> p n h d", h=H),
                                              AX.X, ALU.add).then_inc(k_sum, 1)
                        else:
                            dve.tensor_reduce(logits[:, lt % 2, NN, :], own[:, 0:D].rearrange("p (h d) -> p h d", h=H),
                                              AX.X, ALU.add).then_inc(k_sum, 1)

                    multiply(groups[0])
                    for g in groups[1:]:
                        multiply(g)
                        reduce(g - 1)
                    reduce(groups[-1])

                def shift(b, lt):
                    n = b * TT + lt
                    lg = logits[:, lt % 2]
                    dve.wait_ge(k_sum, START + n * (NG + 1) + NG + 1)
                    dve.tensor_tensor(lg[:, 0:NN, :], lg[:, 0:NN, :],
                                      hide[:, lt, :].unsqueeze(2).to_broadcast([P, NN, H]), ALU.add)\
                        .then_inc(max_step, 1)
                    dve.wait_ge(max_step, START + n * 2 + 1)
                    dve.tensor_reduce(top[:], lg.rearrange("p n h -> p h n"), AX.X, ALU.max).then_inc(max_step, 1)
                    dve.wait_ge(max_step, START + n * 2 + 2)
                    dve.tensor_tensor(lg, lg, top[:].unsqueeze(1).to_broadcast([P, NN + 1, H]), ALU.subtract)\
                        .then_inc(shifted, 1)

                def normalise(b, lt):
                    n = b * TT + lt
                    dve.wait_ge(exp_done, START + n + 1)
                    dve.tensor_reduce(total[:], weights[:].rearrange("p n h -> p h n"), AX.X, ALU.add)\
                        .then_inc(norm_step, 1)
                    dve.wait_ge(norm_step, START + n * 2 + 1)
                    dve.reciprocal(total[:], total[:]).then_inc(norm_step, 1)
                    dve.wait_ge(norm_step, START + n * 2 + 2)
                    dve.tensor_tensor(weights[:], weights[:], total[:].unsqueeze(1).to_broadcast([P, NN + 1, H]),
                                      ALU.mult).then_inc(weights_ready, 1)

                def values(b, lt):
                    n = b * TT + lt
                    o = o_sb[:, lt % 2, :]
                    dve.wait_ge(weights_ready, START + n + 1)

                    def multiply(g):
                        dve.wait_ge(gathered[slot(lt, g)], (16 * GN) * fills(b, lt, g))
                        vv = nb[:, slot(lt, g), :, D:2 * D].rearrange("p n (h d) -> p n h d", h=H)
                        w = weights[:, g * GN:(g + 1) * GN, :].unsqueeze(3).to_broadcast([P, GN, H, DH])
                        dve.tensor_tensor(vv, vv, w, ALU.mult).then_inc(v_mul_dve, 1)

                    def pair(g):
                        if g in POOL_V_GROUPS:
                            dve.wait_ge(v_mul_pool, START + n * len(POOL_V_GROUPS) + POOL_V_GROUPS.index(g) + 1)
                        else:
                            dve.wait_ge(v_mul_dve, START + n * len(DVE_V_GROUPS) + DVE_V_GROUPS.index(g) + 1)
                        v = nb[:, slot(lt, g), :, D:2 * D]
                        dve.tensor_tensor(v[:, 0, :], v[:, 0, :], v[:, 1, :], ALU.add).then_inc(v_pair, 1)

                    def accumulate(g):
                        dve.wait_ge(v_pair, START + n * NG + g + 1)
                        dve.wait_ge(o_part, START + n * (NG + 1) + g + 1)
                        dve.tensor_tensor(o, o, nb[:, slot(lt, g), 0, D:2 * D], ALU.add).then_inc(o_part, 1)

                    multiply(0)
                    dve.tensor_tensor(o.rearrange("p (h d) -> p h d", h=H),
                                      own[:, D:2 * D].rearrange("p (h d) -> p h d", h=H),
                                      weights[:, NN, :].unsqueeze(2).to_broadcast([P, H, DH]), ALU.mult)\
                        .then_inc(o_part, 1)
                    for g in range(NG):
                        if g + 1 in DVE_V_GROUPS:
                            multiply(g + 1)
                        pair(g)
                        if g:
                            accumulate(g - 1)
                    accumulate(NG - 1)

                def norm_stats(j, s, tile):
                    if not isinstance(j, int) or j > 1:
                        dve.wait_ge(ln_out, START + j - 1)
                    dve.bn_stats(stats[:, s, :], tile).then_inc(ln_part, 1)
                    dve.wait_ge(ln_part, START + j + 1)
                    stand_alone(dve)
                    dve.bn_aggr(mean_var[:, s, :], stats[:, s, :]).then_inc(ln_stats, 1)

                def norm_apply(j, s, tile):
                    dve.wait_ge(ln_rstd, START + j + 1)
                    dve.tensor_scalar(tile, tile, mean_var[:, s, 0:1], rstd[:, s:s + 1],
                                      ALU.subtract, ALU.mult).then_inc(ln_out, 1)

                def x2_sum(b, lt):
                    j, s = norm_x2(b, lt), lt % 2
                    if not (isinstance(b, int) and b == 0):
                        dve.wait_ge(x2b_ready, START + (b - 1) * TT + lt + 1)
                    dve.wait_ge(res_ready, START + b * TT + lt + 1)
                    dve.wait_ge(proj_ready, START + proj_o(b, lt) + 1)
                    dve.tensor_tensor(x2[:, lt, :], PROJ[:], x1_res[:], ALU.add).then_inc(out_added, 1)
                    dve.wait_ge(out_added, START + b * TT + lt + 1)
                    norm_stats(j, s, x2[:, lt, :])

                def x2_apply(b, lt):
                    norm_apply(norm_x2(b, lt), lt % 2, x2[:, lt, :])

                def split_x2(b, half):
                    for lt in tiles(half):
                        dve.wait_ge(turn_copied, START + turn_x2(b, lt) + 1)
                        dve.tensor_tensor(x2T_lo[:, :, lt * P:(lt + 1) * P],
                                          X2_TURN[lt % RT][:].rearrange("p (c t) -> p c t", c=KC),
                                          x2T_hi[:, :, lt * P:(lt + 1) * P], ALU.subtract).then_inc(x2_split, 1)

                def output_sum(b, lt):
                    if lt % RT == 0:
                        dve.wait_ge(mlp_ready, START + round_of(b, lt) + 1)
                    dve.wait_ge(x2b_ready, START + b * TT + lt + 1)
                    dve.tensor_tensor(x2b[:, lt, :], ACC[lt][:], x2b[:, lt, :], ALU.add).then_inc(y_added, 1)
                    dve.wait_ge(y_added, START + b * TT + lt + 1)
                    norm_stats(norm_y(b, lt), y_slot(b, lt), x2b[:, lt, :])

                def output_apply(b, lt):
                    norm_apply(norm_y(b, lt), y_slot(b, lt), x2b[:, lt, :])

                def attention(b, half, more):
                    first, second = tiles(half)
                    for lt in (first, second):
                        if lt == first and not is_first(b, lt):
                            key_sums(b, lt, (KEYS_AHEAD,))
                            split_x2(*last_round(b, half))
                            key_sums(b, lt, tuple(range(KEYS_AHEAD + 1, NG + 1)))
                        else:
                            key_sums(b, lt, tuple(range(KEYS_AHEAD, NG + 1)))
                        shift(b, lt)
                        if lt == second:
                            x2_sum(b, first)
                        else:
                            key_sums(b, second, tuple(range(KEYS_AHEAD)))
                        normalise(b, lt)
                        if lt == second:
                            x2_apply(b, first)
                        values(b, lt)
                    if more:
                        nb_, nh = next_round(b, half)
                        key_sums(nb_, nh * RT, tuple(range(KEYS_AHEAD)))
                    if is_first(b, first):
                        x2_sum(b, second)
                    else:
                        yb, yh = last_round(b, half)
                        output_sum(yb, yh * RT)
                        output_sum(yb, yh * RT + 1)
                        output_apply(yb, yh * RT)
                        x2_sum(b, second)
                        output_apply(yb, yh * RT + 1)
                    x2_apply(b, second)

                dve.wait_ge(idx_loaded, START + 16 * 2)
                dve.tensor_copy(idx_f[:], idx_in[:]).then_inc(idx_step, 1)
                dve.wait_ge(idx_step, START + 1)
                dve.tensor_scalar(idx_t[:], idx_f[:], 0.0, float(NODES), ALU.is_lt, ALU.mult).then_inc(idx_step, 1)
                dve.wait_ge(idx_step, START + 2)
                dve.tensor_tensor(idx_f[:], idx_f[:], idx_t[:], ALU.add).then_inc(idx_step, 1)
                dve.wait_ge(idx_step, START + 3)
                dve.tensor_scalar(idx_f[:], idx_f[:], 0.0, float(NODES - 1), ALU.max, ALU.min).then_inc(idx_step, 1)
                dve.tensor_scalar(hide[:], mask_in[:].bitcast(U8), HIDE, None, ALU.mult).then_inc(hide_ready, 1)
                dve.wait_ge(hide_ready, START + 1)
                key_sums(0, 0, tuple(range(KEYS_AHEAD)))
                attention(0, 0, True)
                with dve.Fori(0, B - 1) as b:
                    attention(b, 1, True)
                    attention(b + 1, 0, True)
                attention(B - 1, 1, False)
                split_x2(B - 1, 1)
                output_sum(B - 1, RT)
                output_sum(B - 1, RT + 1)
                output_apply(B - 1, RT)
                output_apply(B - 1, RT + 1)

            @block.gpsimd
            def _(pool):
                def gather(b, i):
                    if i >= TT * NG:
                        b, i = b + 1, i - TT * NG
                    lt, g = i // NG, i % NG
                    if not (isinstance(b, int) and b == 0 and i < SLOTS):
                        pool.wait_ge(o_part, START + summed(b, i - SLOTS))
                        stand_alone(pool)
                    for k in range(GN):
                        at = g * GN + k
                        pool.indirect_dma_start(nb[:, slot(lt, g), k, :], None, kv_flat,
                                                bass.IndirectOffsetOnAxis(idx_rows[:, lt, at:at + 1], 0))\
                            .then_inc(gathered[slot(lt, g)], 16)

                def summed(b, i):
                    if i < 0:
                        b, i = b - 1, i + TT * NG
                    return b * (TT * (NG + 1)) + i // NG * (NG + 1) + i % NG + 2

                def next_rows(b, first, end, step):
                    n = b * ROW_STEPS + step
                    pool.wait_ge(idx_ready, START + n + 1)
                    stand_alone(pool)
                    pool.tensor_scalar(idx_f[:, first:end, :], idx_f[:, first:end, :], float(FLAT), None, ALU.add)\
                        .then_inc(idx_step, 1)
                    pool.wait_ge(idx_step, START + n + 5)
                    stand_alone(pool)
                    pool.tensor_copy(idx_rows[:, first:end, :], idx_f[:, first:end, :]).then_inc(idx_ready, 1)
                    pool.wait_ge(idx_ready, START + n + 2)

                def weight_values(b, lt):
                    pool.wait_ge(weights_ready, START + b * TT + lt + 1)
                    for g in POOL_V_GROUPS:
                        pool.wait_ge(gathered[slot(lt, g)], (16 * GN) * fills(b, lt, g))
                        vv = nb[:, slot(lt, g), :, D:2 * D].rearrange("p n (h d) -> p n h d", h=H)
                        w = weights[:, g * GN:(g + 1) * GN, :].unsqueeze(3).to_broadcast([P, GN, H, DH])
                        pool.tensor_tensor(vv, vv, w, ALU.mult).then_inc(v_mul_pool, 1)

                def residual(b, lt):
                    pool.wait_ge(res_loaded, START + b * (16 * TT) + 16 * (lt + 1))
                    pool.tensor_tensor(x1_res[:], x1_res[:], bo_sb[:], ALU.add).then_inc(res_ready, 1)

                def rstd_of(j, s):
                    pool.wait_ge(ln_stats, START + j + 1)
                    pool.wait_ge(ln_rstd, START + j)
                    stand_alone(pool)
                    pool.tensor_scalar(var_eps[:], mean_var[:, s, 1:2], EPS, None, ALU.add).then_inc(ln_eps, 1)
                    pool.wait_ge(ln_eps, START + j + 2)
                    pool.tensor_tensor(rstd[:, s:s + 1], var_eps[:], half[:], ALU.pow).then_inc(ln_rstd, 1)

                def output_rstds(b, half):
                    for lt in tiles(half):
                        rstd_of(norm_y(b, lt), y_slot(b, lt))

                def residuals2(b, half):
                    pool.wait_ge(out_stored[half], START + b * (16 * RT))
                    for lt in tiles(half):
                        pool.wait_ge(ln_out, START + norm_x2(b, lt) + 1)
                        pool.tensor_tensor(x2b[:, lt, :], x2[:, lt, :], b2_sb[:], ALU.add).then_inc(x2b_ready, 1)

                AHEAD = SLOTS - NG

                def attention(b, half, more):
                    first, second = tiles(half)
                    for lt in (first, second):
                        weight_values(b, lt)
                        if more and lt >= TT - 2:
                            next_rows(b, *((0, 1, 0) if lt == TT - 2 else (1, TT, 1)))
                        for i in range((lt + 1) * NG + AHEAD, (lt + 2) * NG + AHEAD):
                            if more or i < TT * NG:
                                gather(b, i)
                        residual(b, lt)
                        if lt == second and not is_first(b, lt):
                            output_rstds(*last_round(b, half))
                        rstd_of(norm_x2(b, lt), lt % 2)

                pool.memset(half[:], -0.5).then_inc(ln_eps, 1)
                pool.wait_ge(ln_eps, START + 1)
                pool.wait_ge(idx_step, START + 4)
                pool.tensor_copy(idx_rows[:], idx_f[:]).then_inc(idx_ready, 1)
                pool.wait_ge(idx_ready, START + 1)
                for i in range(SLOTS):
                    gather(0, i)
                pool.wait_ge(consts2, START + CONSTS2)
                attention(0, 0, True)
                residuals2(0, 0)
                with pool.Fori(0, B - 1) as b:
                    attention(b, 1, True)
                    residuals2(b, 1)
                    attention(b + 1, 0, True)
                    residuals2(b + 1, 0)
                attention(B - 1, 1, False)
                residuals2(B - 1, 1)
                output_rstds(B - 1, 1)


def rope_tables():
    freq = np.float32(1.0) / np.float32(10000.0) ** (np.arange(0, DH, 2, dtype=np.float32) / np.float32(DH))
    ang = (np.arange(T, dtype=np.float32)[:, None] * freq[None, :]).astype(np.float64)
    d = np.arange(P) % DH
    cos, sin = np.cos(ang)[:, d // 2].T, np.sin(ang)[:, d // 2].T * np.where(d % 2 == 0, -1.0, 1.0)[:, None]
    return np.stack([cos * (SCALE * Q_UP), sin * (SCALE * Q_UP), cos * K_UP, sin * K_UP]).astype(np.float32)


def node_scales():
    s, at, n = np.ones(FLAT, np.float32), T, T // 2
    for level in range(1, LEVELS + 1):
        s[at:at + n] = 0.5 ** level
        at, n = at + n, n // 2
    return np.ascontiguousarray(s.reshape(NT, P).T)


def kernel(x, ctx_1024, itok_Sx12_0_8189, mask_Sx12_bk0, L0_attn_W_qkv, L0_attn_b_qkv, L0_xattn_Wq, L0_xattn_Wk,
           L0_xattn_Wv, L0_xattn_Wo, L0_xattn_bo, L0_ffn_w1, L0_ffn_b1, L0_ffn_w2, L0_ffn_b2):
    import concourse.bacc as bacc
    from concourse.bass_utils import run_bass_kernel_spmd

    x, ctx = np.asarray(x), np.asarray(ctx_1024)
    b_qkv = np.asarray(L0_attn_b_qkv)
    arrays = {
        "x": x, "xT": x.transpose(0, 2, 1), "ctxT": ctx.transpose(0, 2, 1),
        "idx": np.asarray(itok_Sx12_0_8189), "mask": np.ascontiguousarray(mask_Sx12_bk0).view(np.int32),
        "wqkvT": np.asarray(L0_attn_W_qkv).T, "bqk": b_qkv[:2 * D].reshape(2 * KC, P).T, "bv": b_qkv[2 * D:],
        "wkT": np.asarray(L0_xattn_Wk).T, "wvT": np.asarray(L0_xattn_Wv).T, "wqT": np.asarray(L0_xattn_Wq).T,
        "woT": np.asarray(L0_xattn_Wo).T, "bo": np.asarray(L0_xattn_bo),
        "w1": np.asarray(L0_ffn_w1).reshape(KC, P, WIDTH // D, D).transpose(0, 2, 1, 3).reshape(W1_PIECES * P, D),
        "b1": np.asarray(L0_ffn_b1).reshape(WC, P).T,
        "w2": np.asarray(L0_ffn_w2), "b2": np.asarray(L0_ffn_b2),
        "rope": rope_tables(), "node_scale": node_scales(), "ident_in": np.eye(P, dtype=np.float32),
    }
    arrays = {f"in_{k}": np.ascontiguousarray(v) for k, v in arrays.items()}
    nc = bacc.Bacc("TRN2", target_bir_lowering=False, num_devices=1)
    args = [nc.dram_tensor(k, v.shape, mybir.dt.from_np(v.dtype), kind="ExternalInput").ap() for k, v in arrays.items()]
    out = nc.dram_tensor("out", (B, T, D), F32, kind="ExternalOutput").ap()
    decoder_layer(nc, *args, out)
    r = run_bass_kernel_spmd(nc, [arrays], core_ids=[0])
    return r.results[0]["out"]
```
